# Optimizing a Trainium2 kernel written in Bass

```python
import numpy as np
import jax
import jax.numpy as jnp

def _softmax(x, axis=-1):
    return jax.nn.softmax(x, axis=axis)

def _gelu(x):
    return jax.nn.gelu(x, approximate=True)

def _silu(x):
    return jax.nn.silu(x)

def _sigmoid(x):
    return jax.nn.sigmoid(x)

def _layernorm(x, axis=-1, eps=1e-05):
    m = jnp.mean(x, axis=axis, keepdims=True)
    v = jnp.var(x, axis=axis, keepdims=True)
    return (x - m) / jnp.sqrt(v + eps)

def _scatter_add(tgt, idx, src, axis=0):
    return tgt.at[idx].add(src)

def _segment_sum(src, seg, n):
    return jax.ops.segment_sum(src, seg, n)
kernel_name = 'mk_adj_ffn_d2_adj_r2_40633d'

def setup_inputs(seed: int=0):
    np.random.seed(seed)
    _w = jnp.asarray

    def _rec_inputs():
        import jax
        import jax.numpy as jnp
        _gk = jax.random.key(seed)
        x = -0.0002928 + 1 * jax.random.normal(jax.random.fold_in(_gk, 1), (32, 256, 128), jnp.float32)
        _w = (1.0 + jnp.arange(256, dtype=jnp.float32)) ** (-0.5)
        _w = _w / _w.mean()
        _pij = jnp.clip(0.0625 * _w[:, None] * _w[None, :], 0.0, 1.0)
        _a = jax.random.uniform(jax.random.fold_in(_gk, 2), (32, 256, 256)) < _pij
        _a = jnp.logical_or(_a, jnp.swapaxes(_a, -1, -2))
        _a = jnp.logical_or(_a, jnp.eye(256, dtype=bool))
        _af = _a.astype(jnp.float32)
        _af = _af * jax.random.uniform(jax.random.fold_in(_gk, 3), (32, 256, 256), jnp.float32, 0.05, 0.999994)
        adj = _af
        _nm = jnp.ones((32, 256), dtype=bool)
        nodemask = jnp.where(_nm, 1.0, 0.0).astype(jnp.float32)
        return (x, adj, nodemask)
    x, adj, nodemask = _rec_inputs()

    def _L0_gnn_setup():
        import jax, jax.numpy as jnp
        import numpy as np
        EPS = 1e-08
        key = jax.random.key(seed)
        kH, kA, kW = jax.random.split(key, 3)
        B, N, IN, OUT = (32, 256, 128, 128)
        H = jax.random.normal(kH, (B, N, IN), dtype=jnp.float32)
        A = jax.random.uniform(kA, (B, N, N), dtype=jnp.float32)
        mask = jnp.ones((B, N), dtype=jnp.float32)
        W = jax.random.normal(kW, (OUT, IN), dtype=jnp.float32) * (1.0 / np.sqrt(IN))
        b = jnp.zeros((OUT,), dtype=jnp.float32)
        return {'H': H, 'A': A, 'mask': mask, 'W': W, 'b': b}
    _L0_gnn_all = _L0_gnn_setup()
    _L0_gnn_in = {k: v for k, v in _L0_gnn_all.items() if k in ('W', 'b')}
    del _L0_gnn_all

    def _L0_ffn_setup():
        import jax, jax.numpy as jnp
        import numpy as np
        DIM = 128
        HEADS = 8
        NUM_KEYS = 128
        NUM_KV = NUM_KEYS ** 2
        PK_TOPK = 16
        FINAL_TOPK = 16
        DIM_KEY = DIM // 2
        P = 2

        def _pk(x, Wq_pk, pk_keys):
            b, n, _ = x.shape
            q = (x @ Wq_pk).reshape(b, n, P, HEADS, DIM_KEY).transpose(2, 0, 1, 3, 4)
            sim = jnp.einsum('pbnhd,pkhd->pbnhk', q, pk_keys)
            scores, idx = jax.lax.top_k(sim, PK_TOPK)
            idx0 = idx[0]
            idx1 = idx[1] * NUM_KEYS
            index = (idx0[..., :, None] + idx1[..., None, :]).reshape(b, n, HEADS, PK_TOPK * PK_TOPK)
            score = (scores[0][..., :, None] + scores[1][..., None, :]).reshape(b, n, HEADS, PK_TOPK * PK_TOPK)
            final_scores, pk_idx = jax.lax.top_k(score, FINAL_TOPK)
            final_indices = jnp.take_along_axis(index, pk_idx, axis=-1)
            final_scores = jax.nn.softmax(final_scores, axis=-1)
            return (final_scores, final_indices)
        key = jax.random.key(seed)
        ks = jax.random.split(key, 7)
        b, n = (2, 512)
        std = 0.02
        x = jax.random.normal(ks[0], (b, n, DIM), dtype=jnp.float32)
        Wq_pk = jax.random.normal(ks[1], (DIM, P * HEADS * DIM_KEY), dtype=jnp.float32) * std
        pk_keys = jax.random.normal(ks[2], (P, NUM_KEYS, HEADS, DIM_KEY), dtype=jnp.float32) * std
        Wq = jax.random.normal(ks[3], (DIM, HEADS * DIM), dtype=jnp.float32) * std
        keys_table = jax.random.normal(ks[4], (NUM_KV * HEADS, DIM), dtype=jnp.float32) * std
        values_table = jax.random.normal(ks[5], (NUM_KV * HEADS, DIM), dtype=jnp.float32) * std
        Wo = jax.random.normal(ks[6], (DIM * HEADS, DIM), dtype=jnp.float32) * std
        return {'x': x, 'Wq_pk': Wq_pk, 'pk_keys': pk_keys, 'Wq': Wq, 'keys_table': keys_table, 'values_table': values_table, 'Wo': Wo}
    _L0_ffn_all = _L0_ffn_setup()
    _L0_ffn_in = {k: v for k, v in _L0_ffn_all.items() if k in ('Wq_pk', 'pk_keys', 'Wq', 'keys_table', 'values_table', 'Wo')}
    del _L0_ffn_all

    def _L1_gnn_setup():
        import jax, jax.numpy as jnp
        import numpy as np
        B, N, D = (4, 2048, 128)
        DENSITY = 32.0 / N
        key = jax.random.key(seed)
        kx, ka, k1, k2, k3, k4 = jax.random.split(key, 6)
        x = jax.random.normal(kx, (B, N, D), dtype=jnp.float32)
        adj = (jax.random.uniform(ka, (B, N, N)) < DENSITY).astype(jnp.float32)
        scale = 0.02
        theta = scale * jax.random.normal(k1, (D, D), dtype=jnp.float32)
        W_h = scale * jax.random.normal(k2, (D, D), dtype=jnp.float32)
        W_t = scale * jax.random.normal(k3, (D, D), dtype=jnp.float32)
        b_t = scale * jax.random.normal(k4, (D,), dtype=jnp.float32)
        return {'x': x, 'adj': adj, 'theta': theta, 'W_h': W_h, 'W_t': W_t, 'b_t': b_t}
    _L1_gnn_all = _L1_gnn_setup()
    _L1_gnn_in = {k: v for k, v in _L1_gnn_all.items() if k in ('theta', 'W_h', 'W_t', 'b_t')}
    del _L1_gnn_all

    def _L1_ffn_setup():
        import jax, jax.numpy as jnp
        import numpy as np
        H, P, G, NS, K = (8, 64, 64, 64, 3)
        D_INNER = H * P
        CONV_DIM = D_INNER + 2 * NS
        D_IN_PROJ = 2 * D_INNER + 2 * NS + 2 * H

        def _hydra(u, in_w, conv_w, conv_b, dt_bias, A_log, Dp, fcD_w, norm_w, out_w):
            Bt, L, _ = u.shape
            zxbcdt = u @ in_w.T
            z = zxbcdt[..., :D_INNER]
            xBC = zxbcdt[..., D_INNER:D_INNER + CONV_DIM]
            dt = zxbcdt[..., -2 * H:]
            dt = jnp.concatenate([dt[..., :H], jnp.flip(dt[..., H:], axis=1)], axis=0)
            dt = jax.nn.softplus(dt + dt_bias)
            xp = jnp.pad(xBC, ((0, 0), (K - 1, 0), (0, 0)))
            xBC = sum((xp[:, k:k + L, :] * conv_w[:, k] for k in range(K))) + conv_b
            xBC = jax.nn.silu(xBC)
            x = xBC[..., :D_INNER]
            Bm = xBC[..., D_INNER:D_INNER + NS]
            Cm = xBC[..., D_INNER + NS:]
            x_og = x
            x2 = jnp.concatenate([x, jnp.flip(x, 1)], 0).reshape(2 * Bt, L, H, P)
            B2 = jnp.concatenate([Bm, jnp.flip(Bm, 1)], 0)
            C2 = jnp.concatenate([Cm, jnp.flip(Cm, 1)], 0)
            dA = jnp.exp(dt * -jnp.exp(A_log))
            dBx = jnp.einsum('blh,bln,blhp->blhpn', dt, B2, x2)

            def step(h, inp):
                dA_t, dBx_t, C_t = inp
                h = h * dA_t[:, :, None, None] + dBx_t
                return (h, jnp.einsum('bhpn,bn->bhp', h, C_t))
            h0 = jnp.zeros((2 * Bt, H, P, NS), u.dtype)
            _, ys = jax.lax.scan(step, h0, (dA.transpose(1, 0, 2), dBx.transpose(1, 0, 2, 3, 4), C2.transpose(1, 0, 2)))
            y = ys.transpose(1, 0, 2, 3).reshape(2 * Bt, L, D_INNER)
            y_fw, y_bw = (y[:Bt], jnp.flip(y[Bt:], 1))
            y = jnp.pad(y_fw[:, :-1], ((0, 0), (1, 0), (0, 0))) + jnp.pad(y_bw[:, 1:], ((0, 0), (0, 1), (0, 0)))
            y = y + x_og * jnp.repeat(x_og @ fcD_w.T + Dp, P, axis=-1)
            yg = y * jax.nn.silu(z)
            yg = yg * jax.lax.rsqrt(jnp.mean(jnp.square(yg), -1, keepdims=True) + 1e-05) * norm_w
            return yg @ out_w.T
        key = jax.random.key(seed)
        ks = jax.random.split(key, 10)
        dim, Bsz, N = (128, 4, 4096)
        s = 0.02
        return {'x': jax.random.normal(ks[0], (Bsz, N, dim), jnp.float32), 'W_fx': jax.random.normal(ks[1], (D_INNER, dim), jnp.float32) * s, 'b_fx': jnp.zeros((D_INNER,), jnp.float32), 'W_x': jax.random.normal(ks[2], (D_INNER, dim), jnp.float32) * s, 'b_x': jnp.zeros((D_INNER,), jnp.float32), 'W_slice': jax.random.normal(ks[3], (G, P), jnp.float32) * s, 'b_slice': jnp.zeros((G,), jnp.float32), 'temperature': jnp.full((1, H, 1, 1), 0.5, jnp.float32), 'hy_in_w': jax.random.normal(ks[4], (D_IN_PROJ, D_INNER), jnp.float32) * s, 'hy_conv_w': jax.random.normal(ks[5], (CONV_DIM, K), jnp.float32) * s, 'hy_conv_b': jnp.zeros((CONV_DIM,), jnp.float32), 'hy_dt_bias': jnp.log(jnp.expm1(jnp.full((H,), 0.01, jnp.float32))), 'hy_A_log': jnp.log(jnp.linspace(1.0, 16.0, H)).astype(jnp.float32), 'hy_D': jnp.ones((H,), jnp.float32), 'hy_fcD_w': jax.random.normal(ks[6], (H, D_INNER), jnp.float32) * s, 'hy_norm_w': jnp.ones((D_INNER,), jnp.float32), 'hy_out_w': jax.random.normal(ks[7], (D_INNER, D_INNER), jnp.float32) * s, 'out_w': jax.random.normal(ks[8], (dim, D_INNER), jnp.float32) * s, 'out_b': jnp.zeros((dim,), jnp.float32)}
    _L1_ffn_all = _L1_ffn_setup()
    _L1_ffn_in = {k: v for k, v in _L1_ffn_all.items() if k in ('W_fx', 'b_fx', 'W_x', 'b_x', 'W_slice', 'b_slice', 'temperature', 'hy_in_w', 'hy_conv_w', 'hy_conv_b', 'hy_dt_bias', 'hy_A_log', 'hy_D', 'hy_fcD_w', 'hy_norm_w', 'hy_out_w', 'out_w', 'out_b')}
    del _L1_ffn_all
    return {'x': x, 'adj': adj, 'nodemask': nodemask, 'L0_gnn_W': _L0_gnn_in['W'], 'L0_gnn_b': _L0_gnn_in['b'], 'L0_ffn_Wq_pk': _L0_ffn_in['Wq_pk'], 'L0_ffn_pk_keys': _L0_ffn_in['pk_keys'], 'L0_ffn_Wq': _L0_ffn_in['Wq'], 'L0_ffn_keys_table': _L0_ffn_in['keys_table'], 'L0_ffn_values_table': _L0_ffn_in['values_table'], 'L0_ffn_Wo': _L0_ffn_in['Wo'], 'L1_gnn_theta': _L1_gnn_in['theta'], 'L1_gnn_W_h': _L1_gnn_in['W_h'], 'L1_gnn_W_t': _L1_gnn_in['W_t'], 'L1_gnn_b_t': _L1_gnn_in['b_t'], 'L1_ffn_W_fx': _L1_ffn_in['W_fx'], 'L1_ffn_b_fx': _L1_ffn_in['b_fx'], 'L1_ffn_W_x': _L1_ffn_in['W_x'], 'L1_ffn_b_x': _L1_ffn_in['b_x'], 'L1_ffn_W_slice': _L1_ffn_in['W_slice'], 'L1_ffn_b_slice': _L1_ffn_in['b_slice'], 'L1_ffn_temperature': _L1_ffn_in['temperature'], 'L1_ffn_hy_in_w': _L1_ffn_in['hy_in_w'], 'L1_ffn_hy_conv_w': _L1_ffn_in['hy_conv_w'], 'L1_ffn_hy_conv_b': _L1_ffn_in['hy_conv_b'], 'L1_ffn_hy_dt_bias': _L1_ffn_in['hy_dt_bias'], 'L1_ffn_hy_A_log': _L1_ffn_in['hy_A_log'], 'L1_ffn_hy_D': _L1_ffn_in['hy_D'], 'L1_ffn_hy_fcD_w': _L1_ffn_in['hy_fcD_w'], 'L1_ffn_hy_norm_w': _L1_ffn_in['hy_norm_w'], 'L1_ffn_hy_out_w': _L1_ffn_in['hy_out_w'], 'L1_ffn_out_w': _L1_ffn_in['out_w'], 'L1_ffn_out_b': _L1_ffn_in['out_b']}

def reference(x, adj, nodemask, L0_gnn_W, L0_gnn_b, L0_ffn_Wq_pk, L0_ffn_pk_keys, L0_ffn_Wq, L0_ffn_keys_table, L0_ffn_values_table, L0_ffn_Wo, L1_gnn_theta, L1_gnn_W_h, L1_gnn_W_t, L1_gnn_b_t, L1_ffn_W_fx, L1_ffn_b_fx, L1_ffn_W_x, L1_ffn_b_x, L1_ffn_W_slice, L1_ffn_b_slice, L1_ffn_temperature, L1_ffn_hy_in_w, L1_ffn_hy_conv_w, L1_ffn_hy_conv_b, L1_ffn_hy_dt_bias, L1_ffn_hy_A_log, L1_ffn_hy_D, L1_ffn_hy_fcD_w, L1_ffn_hy_norm_w, L1_ffn_hy_out_w, L1_ffn_out_w, L1_ffn_out_b):
    import jax
    import jax.numpy as jnp

    def _L0_gnn_ref(H, A, mask, W, b):
        import jax, jax.numpy as jnp
        import numpy as np
        EPS = 1e-08
        N = A.shape[-1]
        A_hat = A + jnp.eye(N, dtype=A.dtype)
        deg = A_hat.sum(axis=-1)
        dis = (deg + EPS) ** (-0.5)
        A_norm = dis[:, :, None] * A_hat * dis[:, None, :]
        H_lin = jnp.einsum('bni,oi->bno', H, W) + b
        out = jnp.einsum('bnm,bmo->bno', A_norm, H_lin)
        out = out * mask[:, :, None]
        return jax.nn.relu(out)

    def _L0_ffn_ref(x, Wq_pk, pk_keys, Wq, keys_table, values_table, Wo):
        import jax, jax.numpy as jnp
        import numpy as np
        DIM = 128
        HEADS = 8
        NUM_KEYS = 128
        NUM_KV = NUM_KEYS ** 2
        PK_TOPK = 16
        FINAL_TOPK = 16
        DIM_KEY = DIM // 2
        P = 2

        def _pk(x, Wq_pk, pk_keys):
            b, n, _ = x.shape
            q = (x @ Wq_pk).reshape(b, n, P, HEADS, DIM_KEY).transpose(2, 0, 1, 3, 4)
            sim = jnp.einsum('pbnhd,pkhd->pbnhk', q, pk_keys)
            scores, idx = jax.lax.top_k(sim, PK_TOPK)
            idx0 = idx[0]
            idx1 = idx[1] * NUM_KEYS
            index = (idx0[..., :, None] + idx1[..., None, :]).reshape(b, n, HEADS, PK_TOPK * PK_TOPK)
            score = (scores[0][..., :, None] + scores[1][..., None, :]).reshape(b, n, HEADS, PK_TOPK * PK_TOPK)
            final_scores, pk_idx = jax.lax.top_k(score, FINAL_TOPK)
            final_indices = jnp.take_along_axis(index, pk_idx, axis=-1)
            final_scores = jax.nn.softmax(final_scores, axis=-1)
            return (final_scores, final_indices)
        b, n, d = x.shape
        q = (x @ Wq).reshape(b, n, HEADS, DIM) * DIM ** (-0.5)
        kv_scores, indices = _pk(x, Wq_pk, pk_keys)
        offsets = jnp.arange(HEADS, dtype=indices.dtype) * NUM_KV
        ind = indices + offsets[None, None, :, None]
        k = jnp.einsum('bnhk,bnhkd->bnhd', kv_scores, keys_table[ind])
        v = jnp.einsum('bnhk,bnhkd->bnhd', kv_scores, values_table[ind])
        sim = jnp.einsum('bihd,bjhd->bhij', q, k)
        neg = -jnp.finfo(sim.dtype).max
        causal = jnp.tril(jnp.ones((n, n), dtype=bool))
        sim = jnp.where(causal, sim, neg)
        attn = jax.nn.softmax(sim, axis=-1)
        out = jnp.einsum('bhij,bjhd->bhid', attn, v)
        out = out.transpose(0, 2, 1, 3).reshape(b, n, HEADS * DIM)
        return out @ Wo

    def _L1_gnn_ref(x, adj, theta, W_h, W_t, b_t):
        import jax, jax.numpy as jnp
        import numpy as np
        B, N, D = (4, 2048, 128)
        DENSITY = 32.0 / N
        in_degrees = jnp.sum(jnp.abs(adj), axis=-1)
        norm = ((in_degrees + 1e-06) ** (-0.5))[..., None]
        f_hom = jnp.einsum('bnd,de->bne', x, theta) * norm
        f_hom = jnp.einsum('bnm,bmd->bnd', adj, f_hom) * norm
        f_het = jnp.einsum('bnd,de->bne', x, W_h)
        gate = jax.nn.sigmoid(jnp.einsum('bnd,de->bne', x, W_t) + b_t)
        out = gate * f_hom + (1.0 - gate) * f_het
        return jax.nn.elu(out)

    def _L1_ffn_ref(x, W_fx, b_fx, W_x, b_x, W_slice, b_slice, temperature, hy_in_w, hy_conv_w, hy_conv_b, hy_dt_bias, hy_A_log, hy_D, hy_fcD_w, hy_norm_w, hy_out_w, out_w, out_b):
        import jax, jax.numpy as jnp
        import numpy as np
        H, P, G, NS, K = (8, 64, 64, 64, 3)
        D_INNER = H * P
        CONV_DIM = D_INNER + 2 * NS
        D_IN_PROJ = 2 * D_INNER + 2 * NS + 2 * H

        def _hydra(u, in_w, conv_w, conv_b, dt_bias, A_log, Dp, fcD_w, norm_w, out_w):
            Bt, L, _ = u.shape
            zxbcdt = u @ in_w.T
            z = zxbcdt[..., :D_INNER]
            xBC = zxbcdt[..., D_INNER:D_INNER + CONV_DIM]
            dt = zxbcdt[..., -2 * H:]
            dt = jnp.concatenate([dt[..., :H], jnp.flip(dt[..., H:], axis=1)], axis=0)
            dt = jax.nn.softplus(dt + dt_bias)
            xp = jnp.pad(xBC, ((0, 0), (K - 1, 0), (0, 0)))
            xBC = sum((xp[:, k:k + L, :] * conv_w[:, k] for k in range(K))) + conv_b
            xBC = jax.nn.silu(xBC)
            x = xBC[..., :D_INNER]
            Bm = xBC[..., D_INNER:D_INNER + NS]
            Cm = xBC[..., D_INNER + NS:]
            x_og = x
            x2 = jnp.concatenate([x, jnp.flip(x, 1)], 0).reshape(2 * Bt, L, H, P)
            B2 = jnp.concatenate([Bm, jnp.flip(Bm, 1)], 0)
            C2 = jnp.concatenate([Cm, jnp.flip(Cm, 1)], 0)
            dA = jnp.exp(dt * -jnp.exp(A_log))
            dBx = jnp.einsum('blh,bln,blhp->blhpn', dt, B2, x2)

            def step(h, inp):
                dA_t, dBx_t, C_t = inp
                h = h * dA_t[:, :, None, None] + dBx_t
                return (h, jnp.einsum('bhpn,bn->bhp', h, C_t))
            h0 = jnp.zeros((2 * Bt, H, P, NS), u.dtype)
            _, ys = jax.lax.scan(step, h0, (dA.transpose(1, 0, 2), dBx.transpose(1, 0, 2, 3, 4), C2.transpose(1, 0, 2)))
            y = ys.transpose(1, 0, 2, 3).reshape(2 * Bt, L, D_INNER)
            y_fw, y_bw = (y[:Bt], jnp.flip(y[Bt:], 1))
            y = jnp.pad(y_fw[:, :-1], ((0, 0), (1, 0), (0, 0))) + jnp.pad(y_bw[:, 1:], ((0, 0), (0, 1), (0, 0)))
            y = y + x_og * jnp.repeat(x_og @ fcD_w.T + Dp, P, axis=-1)
            yg = y * jax.nn.silu(z)
            yg = yg * jax.lax.rsqrt(jnp.mean(jnp.square(yg), -1, keepdims=True) + 1e-05) * norm_w
            return yg @ out_w.T
        B, N, _ = x.shape
        fx = (x @ W_fx.T + b_fx).reshape(B, N, H, P).transpose(0, 2, 1, 3)
        xm = (x @ W_x.T + b_x).reshape(B, N, H, P).transpose(0, 2, 1, 3)
        temp = jnp.maximum(temperature, 1e-06)
        sw = jax.nn.softmax((xm @ W_slice.T + b_slice) / temp, axis=-1)
        snorm = sw.sum(2)
        st = jnp.einsum('bhnc,bhng->bhgc', fx, sw) / (snorm + 1e-05)[..., None]
        st = st.transpose(0, 2, 1, 3).reshape(B, G, D_INNER)
        ot = _hydra(st, hy_in_w, hy_conv_w, hy_conv_b, hy_dt_bias, hy_A_log, hy_D, hy_fcD_w, hy_norm_w, hy_out_w)
        ot = ot.reshape(B, G, H, P).transpose(0, 2, 1, 3)
        out = jnp.einsum('bhgc,bhng->bhnc', ot, sw).transpose(0, 2, 1, 3).reshape(B, N, D_INNER)
        return out @ out_w.T + out_b
    x = x + _L0_gnn_ref(_layernorm(x, axis=-1), adj, nodemask, L0_gnn_W, L0_gnn_b)
    x = x + _L0_ffn_ref(_layernorm(x, axis=-1), L0_ffn_Wq_pk, L0_ffn_pk_keys, L0_ffn_Wq, L0_ffn_keys_table, L0_ffn_values_table, L0_ffn_Wo)
    x = x + _L1_gnn_ref(_layernorm(x, axis=-1), adj, L1_gnn_theta, L1_gnn_W_h, L1_gnn_W_t, L1_gnn_b_t)
    x = x + _L1_ffn_ref(_layernorm(x, axis=-1), L1_ffn_W_fx, L1_ffn_b_fx, L1_ffn_W_x, L1_ffn_b_x, L1_ffn_W_slice, L1_ffn_b_slice, L1_ffn_temperature, L1_ffn_hy_in_w, L1_ffn_hy_conv_w, L1_ffn_hy_conv_b, L1_ffn_hy_dt_bias, L1_ffn_hy_A_log, L1_ffn_hy_D, L1_ffn_hy_fcD_w, L1_ffn_hy_norm_w, L1_ffn_hy_out_w, L1_ffn_out_w, L1_ffn_out_b)
    return x

_drawn_inputs = setup_inputs


def setup_inputs(seed=0):
    import zlib

    import numpy as np

    out = dict(_drawn_inputs(seed))
    spreads = {'L0_gnn_b': (0.0, 0.1),
     'L1_ffn_b_fx': (0.0, 0.1),
     'L1_ffn_b_x': (0.0, 0.8),
     'L1_ffn_b_slice': (0.0, 0.8),
     'L1_ffn_temperature': (0.5, 0.6),
     'L1_ffn_hy_conv_b': (0.0, 0.1),
     'L1_ffn_hy_dt_bias': (-4.600166320800781, 0.6),
     'L1_ffn_hy_D': (1.0, 0.6),
     'L1_ffn_hy_norm_w': (1.0, 0.6),
     'L1_ffn_out_b': (0.0, 0.1)}
    factors = {'L0_ffn_Wq_pk': 8.0,
     'L0_ffn_pk_keys': 8.0,
     'L0_ffn_Wq': 64.0,
     'L0_ffn_keys_table': 64.0,
     'L0_ffn_values_table': 8.0,
     'L0_ffn_Wo': 8.0,
     'L1_gnn_W_t': 4.793,
     'L1_gnn_b_t': 47.939,
     'L1_ffn_W_fx': 3.713,
     'L1_ffn_W_x': 8.0,
     'L1_ffn_W_slice': 8.0,
     'L1_ffn_hy_conv_w': 8.0,
     'L1_ffn_hy_A_log': 64.0,
     'L1_ffn_hy_fcD_w': 26.523}
    for name, (base, spread) in spreads.items():
        noise = np.random.default_rng([zlib.crc32(name.encode()), seed]).standard_normal(out[name].shape)
        drawn = base * np.exp(spread * noise) if base else spread * noise
        out[name] = jnp.asarray(drawn.astype(out[name].dtype))
    for name, factor in factors.items():
        out[name] = (out[name] * factor).astype(out[name].dtype)
    return out
```

```python
import concourse.bass as bass
from concourse import mybir
from contextlib import ExitStack


FIRST_ACT = "FFFFFFFFFFFFFGGGGGGF"
FIRST_PE = "FFFFFFFFFFFGGGGGG"
FIRST_DVE = "FFFFFFFFFFFFFFFFFFFFFFFFFFFHFFFFFFFFFFGFFFFFFGFFFFGFFH"
ORDER_ACT = "GGBBBGBBBFFGFBGBGBFGBFFGBFFGBFGGBFBGBGGBBGGBGFGBGBBGBGFBGGFGBBBGGBGBBGGBBGBGGBBF"
LAST_ACT = "GGBBBGBBBGBBGBGBGBGBGBGBGBGBGBGGBGBBGBGBGBGGGBBBGBGBBGBBGBGGGBGBGG"
ORDER_PE = "GBGBBBFBGFGFBGBFBGBFGBFFBFBGBFGBGFBGBGBGGBBBGBGBGBGGBBGGFBGGGBBGGGGBGBGBGBGBBB"
LAST_PE = "GBGBBBGBGBBBGBGBGBBGBGBGBBGBGBGBBGBGBGBGBGBGBGGBGBGGBGBGBGBBGBGBGGG"
ORDER_DVE = "BFFFGBGBFFBBBGBBGFBFFFFGFFBFFFGFBFBGFBFBBFFFFFGBBBBGFFBFBGFHFBGFFFGFFFFFFFBGBBFFBFBFGGBFBFFGFFFHB"
LAST_DVE = "BGBBGBBBGBGBBGBBBGBBBGBGBBBGBBBGGBBBGBBGBBGBGG"


def build_program(nc, x, adj, nodemask, tables, w0T, b0, wqpk, keysT, wq, wo, w1, bt,
                  wx, bx, wsliceT, bslice, temp, wfxT, bfx, inT, convw, convb, dtb, alog,
                  drep, fcdT, normw, houtT, outT, outb, out):
    f32, u32, i32 = mybir.dt.float32, mybir.dt.uint32, mybir.dt.int32
    ALU, ACT = mybir.AluOpType, mybir.ActivationFunctionType
    X = mybir.AxisListType.X

    NB, N, D = x.shape
    P = 128
    T = N // P
    H = 8
    K = 16
    NKEYS = 128
    NKV = NKEYS * NKEYS
    ROW = 2 * D
    CH = T * H
    PARTS = 2
    KP = K // PARTS
    RING = 4
    G = 64
    HD = 64
    DI = H * HD
    KC = DI // P
    NZX = 2 * DI + 2 * HD + 2 * H
    WIDTH = [K // (i + 1) for i in range(K)]
    START = [sum(WIDTH[:i]) for i in range(K)]
    NC = sum(WIDTH)
    LOWEST = -3.0e38
    SCALE = float(D) ** -0.5
    NFRONT, NLOADS = 4, 22
    NPOOL = 22

    ctx = ExitStack()
    with ctx:
        def sb(name, shape, dt=f32):
            return ctx.enter_context(nc.sbuf_tensor(name, shape, dt))

        ident = sb("ident", [P, P])
        ones = sb("ones", [P, P])
        causal = sb("causal", [P, 3, P])
        maskR = sb("maskR", [P, G])
        segL = sb("segL", [P, P])
        maskE = sb("maskE", [P, G])
        iota = sb("iota", [P, NC])
        hoff = sb("hoff", [P, H])
        w0T_s = sb("w0T_s", [P, D])
        wqpk_s = sb("wqpk_s", [P, 2 * H * HD])
        keys_s = sb("keys_s", [P, H, NKEYS])
        wq_s = sb("wq_s", [P, H * D])
        wo_s = sb("wo_s", [P, H, D])
        w1_s = sb("w1_s", [P, 3 * D])
        ws_s = sb("ws_s", [P, DI])
        wfx_s = sb("wfx_s", [P, DI])
        in_s = sb("in_s", [P, KC, NZX])
        fcd_s = sb("fcd_s", [P, KC, DI])
        hout_s = sb("hout_s", [P, KC, DI])
        out_s = sb("out_s", [P, KC, D])
        rows = sb("rows", [65, DI])
        sl_r, bfx_r = rows[0:1, :], rows[32:33, :]
        b0_r, bt_r, ob_r = (rows[64:65, i * D:(i + 1) * D] for i in range(3))
        cw = sb("cw", [P, KC + 2, 3])
        cb = sb("cb", [P, KC + 2])
        dtb_s = sb("dtb_s", [P, H])
        roota = sb("roota", [P, H])
        drep_s = sb("drep_s", [P, KC])
        nw_s = sb("nw_s", [P, KC])
        rtemp = sb("rtemp", [P, H])

        ring = sb("ring", [P, RING, KP, ROW])
        idx_next = sb("idx_next", [P, T, H * K], u32)
        idx_cur = sb("idx_cur", [P, T, H * K], u32)
        w_next = sb("w_next", [P, T, H * K])
        w_cur = sb("w_cur", [P, T, H * K])
        kv_acc = sb("kv_acc", [P, T, H, ROW])
        kv_c = sb("kv_c", [P, T, H, ROW])

        xa = sb("xa", [P, T, D])
        adja = sb("adja", [P, T, N])
        mska = sb("mska", [P, T])
        sta = sb("sta", [P, T, 6])
        mva = sb("mva", [P, T, 2])
        va = sb("va", [P, 4])
        ra = sb("ra", [P, 4])
        rta = sb("rta", [P, 4])
        xna = sb("xna", [P, T, D])
        x1a = sb("x1a", [P, T, D])
        x1Ta = sb("x1Ta", [P, N])
        x1m = sb("x1m", [P, T, D])
        x1Tm = sb("x1Tm", [P, N])
        qp = sb("qp", [P, H, N])
        sim = sb("sim", [P, 2 * H, NKEYS])
        tv = sb("tv", [P, 2 * H, K])
        ti = sb("ti", [P, 2 * H, K], u32)
        tf = sb("tf", [P, 2 * H, K])
        cand = sb("cand", [P, H, NC])
        cidx = sb("cidx", [P, H, NC])
        fv = sb("fv", [P, H, K])
        fp = sb("fp", [P, H, K], u32)
        fpf = sb("fpf", [P, H, K])
        fidx = sb("fidx", [P, H, K])
        fs = sb("fs", [P, H])

        x1c = sb("x1c", [P, T, D])
        x1Tc = sb("x1Tc", [P, N])
        adjc = sb("adjc", [P, T, N])
        qT = sb("qT", [P, H, N])
        mxc = sb("mxc", [P, 4])
        rsc = sb("rsc", [P, 4])
        oT = sb("oT", [P, H, N])
        x2 = sb("x2", [P, T, D])
        stc = sb("stc", [P, T, 6])
        mvc = sb("mvc", [P, T, 2])
        vc = sb("vc", [P, G])
        rc = sb("rc", [P, G])
        rtc = sb("rtc", [P, G])
        xnc = sb("xnc", [P, T, D])
        xnTc = sb("xnTc", [P, N])
        x3 = sb("x3", [P, T, D])
        smx = sb("smx", [P, T * H])
        xp = sb("xp", [P, KC + 2, G + 2])
        yz = sb("yz", [P, 2 * KC + 2, G])
        dtx = sb("dtx", [P, H])
        dte = sb("dte", [P, H])
        dtz = sb("dtz", [P, H])
        dtq = sb("dtq", [P, H])
        dtp = sb("dtp", [P, H])
        dts = sb("dts", [P, H])
        da = sb("da", [P, H])
        cbm = sb("cbm", [P, G])
        Mp = sb("Mp", [P, H, G + 2])
        res = sb("res", [P, T, D])

        def place(buf, at, n):
            return buf[:, at:at + n]

        kv_flat = kv_c[:, :, :, :].rearrange("p t h r -> p (t h r)")
        oT_flat = oT[:, :, :].rearrange("p h n -> p (h n)")
        sw = place(kv_flat, 0, T * H * G).rearrange("p (t h g) -> p t h g", h=H, g=G)
        sxn, srcp, sfr, xN = (place(kv_flat, T * H * G + i * DI, DI) for i in range(4))
        vv = place(kv_flat, T * H * G + 4 * DI, KC * D).rearrange("p (k d) -> p k d", d=D)
        E = place(kv_flat, T * H * G + 4 * DI + KC * D, H * G).rearrange("p (h g) -> p h g", g=G)
        NZ = (2 * KC + 2) * G
        ez = place(oT_flat, 0, NZ).rearrange("p (k g) -> p k g", g=G)
        ct = place(oT_flat, NZ, (KC + 2) * G).rearrange("p (k g) -> p k g", g=G)
        xcd = place(oT_flat, NZ + (KC + 2) * G, KC * 2 * G).rearrange("p (k e g) -> p k e g", e=2, g=G)
        rda = place(oT_flat, NZ + (3 * KC + 2) * G, H * G).rearrange("p (h g) -> p h g", g=G)

        att = sb("att", [P, 2048])
        att_flat = att[:, :]
        kT = place(att_flat, 0, 2 * N).rearrange("p (e n) -> p e n", n=N)
        sm = place(att_flat, 2 * N, 6 * P).rearrange("p (e s n) -> p e s n", e=2, s=3)
        pT = place(att_flat, 2 * N + 6 * P, 6 * P).rearrange("p (e s n) -> p e s n", e=2, s=3)
        ATc = place(att_flat, 0, T * N).rearrange("p (m n) -> p m n", n=N)
        fh, het, gate, g1, g2 = (place(att_flat, (2 + i) * N, T * D).rearrange("p (t d) -> p t d", d=D)
                                 for i in range(5))
        absj = place(att_flat, 7 * N, N)
        uT, yg, sq, otT = (place(att_flat, i * KC * G, KC * G).rearrange("p (k g) -> p k g", g=G)
                           for i in range(4))
        bd = att[0:HD, 4 * KC * G:4 * KC * G + 2 * G].rearrange("p (e g) -> p e g", g=G)
        qp_flat = qp[:, :, :].rearrange("p h n -> p (h n)")
        ATa = place(qp_flat, 0, T * N).rearrange("p (m n) -> p m n", n=N)
        hsa = place(qp_flat, T * N, T * D).rearrange("p (t d) -> p t d", d=D)
        xnTa = place(qp_flat, T * N + T * D, N)
        hot = place(sim[:, :, :].rearrange("p r k -> p (r k)"), 0, K * NC).rearrange("p (k c) -> p k c", c=NC)

        bank = [ctx.enter_context(nc.psum_tensor(f"bank{i}", [P, 512], f32)) for i in range(5)]
        wide = ctx.enter_context(nc.psum_tensor("wide", [P, 3, 512], f32))
        pk, pm, pn = wide[:, 0, :], wide[:, 1, :], wide[:, 2, :]
        pmn = wide[:, 1:3, :]

        def v3(ap, a, b):
            return ap.rearrange("p (a b) -> p a b", b=b)[:, 0:a, :]

        swT = qT[:, 0:KC, :]

        PER_BATCH = dict(
            f_loaded=48, f_xn=1, f_xnT_ps=1, f_xnT=1, f_hlin_ps=1, f_hs=1, f_adjT_ps=1, f_adjT=1,
            f_agg_ps=1, f_x1=1, f_x1n=1, f_x1nT_ps=1, f_x1nT=1, f_qp_ps=4, f_qp=4,
            f_sim_ps=4, f_sim=4, f_sim_used=2, f_fs=2, f_exp=2, f_weights=2, f_mid=1,
            idx_ready=2, part_scaled=PARTS * CH, part_added=PARTS * CH, chunk_saved=CH,
            c_snap=1, c_qT_ps=4, c_qT=4, c_kT_ps=4, c_kT=4, c_sim_ps=4, c_sm=4, c_exp=4, c_prob=4,
            c_pT_ps=4, c_pT=4, c_oT_ps=4, c_oT=4, c_wo_ps=1, c_x2=1, c_adj=16, c_xn2=1,
            c_xn2T_ps=1, c_xn2T=1, c_proj_ps=1, c_fh=1, c_eg=1, c_het=1, c_adjT_ps=1, c_adjT=1,
            c_hom_ps=1, c_neg=1, c_elu=1, c_xn3=1, c_xn3T_ps=1, c_xn3T=1, c_log_ps=1, c_sm3=1,
            c_swe=1, c_sw=1, c_sx_ps=1, c_sxn=1, c_uT_ps=1, c_uT=1, c_swT_ps=2, c_swT=2,
            c_inp_ps=1, c_xp=1, c_dtn=1, c_dte=1, c_conv=1, c_cexp=1, c_xc=1, c_xcd=1,
            c_cb_ps=1, c_rda=1, c_seg_ps=1, c_E=1, c_M=1, c_xN_ps=1, c_xN=1, c_y_ps=1,
            c_sq=1, c_ms_ps=1, c_yn=1, c_ot_ps=1, c_ot=1, c_v_ps=1, c_vv=1, c_out_ps=1,
            c_res=1, stored=16,
        )
        S = {name: ctx.enter_context(nc.semaphore(name)) for name in PER_BATCH}
        for name in ("w_front", "w_loaded", "s_pool", "s_act", "s_pe", "s_dve_a", "s_dve_w", "dve_step",
                     "pool_turn", "dve_turn", "pe_turn"):
            S[name] = ctx.enter_context(nc.semaphore(name))
        arrived = [ctx.enter_context(nc.semaphore(f"arrived{i}")) for i in range(RING)]
        block = ctx.enter_context(nc.Block())

        def after(b, first):
            return not isinstance(b, int) or b > first

        def run_batches(eng, first, order, last, setup, front, gather, back,
                        opening=None, handover=None, closing=None):
            def take_turns(letters, F=iter(()), B=iter(()), G=iter(()), H=iter(())):
                for letter in letters:
                    next(dict(F=F, B=B, G=G, H=H)[letter], None)

            def nothing_left(*stages):
                assert all(next(stage, END) is END for stage in stages), "turns are missing"
                if closing:
                    closing()

            END = object()
            hand = handover or (lambda b: iter(()))
            F, G, H = front(0), gather(0), hand(0)
            take_turns(first, F=F, G=G, H=H)
            assert next(F, END) is END and next(H, END) is END, "turns are missing"
            setup()
            if opening:
                opening(0, False)
            F, H = front(1), hand(1)
            take_turns(order.replace("G", "", first.count("G") // 3), F=F, G=G, H=H)
            nothing_left(F, G, H)
            with eng.Fori(1, NB - 1) as i:
                if opening:
                    opening(i, True)
                F, B, G, H = front(i + 1), back(i - 1), gather(i), hand(i + 1)
                take_turns(order, F=F, B=B, G=G, H=H)
                nothing_left(F, B, G, H)
            if opening:
                opening(NB - 1, True)
            B, G = back(NB - 2), gather(NB - 1)
            take_turns(last, B=B, G=G)
            nothing_left(B, G)
            if opening:
                opening(NB, True)
            for _ in back(NB - 1):
                pass

        counted = dict(steps=0)

        def step():
            counted["steps"] += 1
            return 1

        def steps():
            return counted["steps"]

        def restart(dve):
            dve.wait_ge(S["dve_step"], steps())
            dve.sem_clear(S["dve_step"])
            counted["steps"] = 0

        @block.sync
        def _(sp):
            def load_front(b):
                if after(b, 0):
                    sp.wait_ge(S["f_x1"], b)
                if after(b, 0):
                    sp.wait_ge(S["f_adjT_ps"], b)
                sp.dma_start(xa[:, :, :], x[b, :, :].rearrange("(t p) d -> p t d", p=P)).then_inc(S["f_loaded"], 16)
                sp.dma_start(adja[:, :, :],
                             adj[b, :, :].rearrange("(t p) d -> p t d", p=P)).then_inc(S["f_loaded"], 16)
                sp.dma_start(mska[:, :], nodemask[b, :, :]).then_inc(S["f_loaded"], 16)

            def load_back(b):
                if after(b, 0):
                    sp.wait_ge(S["c_adjT_ps"], b)
                if after(b, 0):
                    sp.wait_ge(S["c_xn2"], b)
                sp.dma_start(adjc[:, :, :], adj[b, :, :].rearrange("(t p) d -> p t d", p=P)).then_inc(S["c_adj"], 16)

            def store(b):
                sp.wait_ge(S["c_res"], b + 1)
                sp.dma_start(out[b, :, :].rearrange("(t p) d -> p t d", p=P), res[:, :, :]).then_inc(S["stored"], 16)

            load_front(0)
            front_loads = [(w0T_s[:, :], w0T), (b0_r, b0), (wqpk_s[:, :], wqpk), (keys_s[:, :, :], keysT)]
            for dst, src in front_loads:
                sp.dma_start(dst, src).then_inc(S["w_front"], 16)
            loads = [
                (wq_s[:, :], wq),
                (wo_s[:, :, :], wo.rearrange("(h p) n -> p h n", p=P)), (w1_s[:, :], w1),
                (wfx_s[:, :], wfxT), (in_s[:, :, :], inT.rearrange("(k p) n -> p k n", p=P)),
                (fcd_s[:, :, :], fcdT.rearrange("(k p) n -> p k n", p=P)),
                (hout_s[:, :, :], houtT.rearrange("(k p) n -> p k n", p=P)),
                (out_s[:, :, :], outT.rearrange("(k p) n -> p k n", p=P)),
                (bt_r, bt), (ob_r, outb), (bfx_r, bfx), (oT[0:1, 4, 0:G], bslice),
                (cw[:, :, :], convw), (cb[:, :], convb),
                (dtb_s[:, :], dtb.to_broadcast([P, H])), (roota[:, :], alog.to_broadcast([P, H])),
                (drep_s[:, :], drep), (nw_s[:, :], normw),
                (rtemp[:, :], temp.to_broadcast([P, H])),
                (oT[:, 0:4, 0:D], wx.rearrange("(k p) n -> p k n", p=P)), (sxn[:, 0:G], wsliceT),
                (sxn[:, G:G + KC], bx),
            ]
            for dst, src in loads:
                sp.dma_start(dst, src).then_inc(S["w_loaded"], 16)
            assert len(front_loads) == NFRONT and len(loads) == NLOADS
            load_front(1)
            load_back(0)
            load_front(2)
            with sp.Fori(1, NB - 2) as i:
                load_front(i + 2)
                store(i - 1)
                load_back(i)
            for i in (NB - 2, NB - 1):
                store(i - 1)
                load_back(i)
            store(NB - 1)
            sp.wait_ge(S["stored"], NB * 16)
            sp.wait_ge(S["pool_turn"], NB * (CH * PARTS + T))
            sp.wait_ge(S["dve_turn"], NB * T * 2)
            sp.wait_ge(S["pe_turn"], NB)

        @block.gpsimd
        def _(pool):
            done = 0

            def fill(ap, value):
                nonlocal done
                if done:
                    pool.wait_ge(S["s_pool"], done)
                pool.memset(ap, value).then_inc(S["s_pool"], 1)
                done += 1

            def choose(ap, pattern, op, value, base, mult):
                nonlocal done
                pool.wait_ge(S["s_pool"], done)
                pool.affine_select(out=ap, in_=ap, compare_op=op, fill=value, base=base,
                                   pattern=pattern, channel_multiplier=mult).then_inc(S["s_pool"], 1)
                done += 1

            fill(ident[:, :], 0.0)
            choose(ident[:, :], [[-1, P]], ALU.not_equal, 1.0, 0, 1)
            fill(ones[:, :], 1.0)
            fill(causal[:, :, :], 0.0)
            for t in (0, 2):
                choose(causal[:, t, :], [[-1, P]], ALU.is_ge, LOWEST, 0, 1)
            fill(segL[:, :], 0.0)
            fill(maskR[:, :], 1.0)
            fill(maskE[:, :], 1.0)
            fill(segL[0:G, 0:G], 1.0)
            fill(segL[G:P, G:P], 1.0)
            choose(segL[0:G, 0:G], [[-1, G]], ALU.is_gt, 0.0, 0, 1)
            choose(segL[G:P, G:P], [[1, G]], ALU.is_gt, 0.0, 0, -1)
            for m in (maskR, maskE):
                choose(m[0:G, :], [[1, G]], ALU.is_ge, 0.0, 0, -1)
                choose(m[G:P, :], [[-1, G]], ALU.is_ge, 0.0, 0, 1)
            for row, stride, length in ((iota, 1, NC), (hoff, NKV // 16, H)):
                pool.wait_ge(S["s_pool"], done)
                pool.iota(row[:, :], pattern=[[stride, length]], base=0, channel_multiplier=0,
                          allow_small_or_imprecise_dtypes=True).then_inc(S["s_pool"], 1)
                done += 1
            fill(xp[:, :, :], 0.0)
            fill(yz[:, :, :], 0.0)
            fill(Mp[:, :, :], 0.0)
            assert done == NPOOL, done

            def gather_batch(b):
                for j in range(CH):
                    t, h = divmod(j, H)
                    if h == 0:
                        pool.wait_ge(S["idx_ready"], b * 2 + (t + 1))
                        pool.sem_inc(S["pool_turn"], 1)
                    for part in range(PARTS):
                        n = PARTS * j + part
                        value = b * CH * PARTS + (n + 1 - RING)
                        if not (isinstance(value, int) and value <= 0):
                            pool.wait_ge(S["part_added"], value)
                        pool.sem_inc(S["pool_turn"], 1)
                        for k in range(KP):
                            s = h * K + part * KP + k
                            pool.indirect_dma_start(
                                out=ring[:, n % RING, k, :], out_offset=None, in_=tables,
                                in_offset=bass.IndirectOffsetOnAxis(ap=idx_cur[:, t, s:s + 1], axis=0),
                            ).then_inc(arrived[n % RING], 16)

            gather_batch(0)
            with pool.Fori(1, NB) as i:
                gather_batch(i)

        @block.scalar
        def _(act):
            def setup():
                act.wait_ge(S["s_dve_a"], 1)
                act.activation(roota[:, :], roota[:, :], ACT.Exp).then_inc(S["s_act"], 1)

            def copy(dst, src):
                return act.activation(dst, src, ACT.Copy)

            def gather(b):
                for n in range(CH * PARTS):
                    t, h, part = n // (H * PARTS), n // PARTS % H, n % PARTS
                    act.wait_ge(S["idx_ready"], b * 2 + (t + 1))
                    full = 16 * KP
                    act.wait_ge(arrived[n % RING], b * (CH * PARTS // RING * full) + (n // RING + 1) * full)
                    for k in range(KP):
                        s = h * K + part * KP + k
                        last = act.activation(ring[:, n % RING, k, :], ring[:, n % RING, k, :], ACT.Copy,
                                              scale=w_cur[:, t, s:s + 1])
                    last.then_inc(S["part_scaled"], 1)
                    yield

            def front(b):
                act.wait_ge(S["f_xnT_ps"], b + 1)
                if after(b, 0):
                    act.wait_ge(S["f_sim_ps"], b * 4)
                copy(xnTa[:, :], bank[2][:, 0:N]).then_inc(S["f_xnT"], 1)
                yield
                act.wait_ge(S["f_adjT_ps"], b + 1)
                copy(ATa[:, :, :], v3(bank[4], T, N)).then_inc(S["f_adjT"], 1)
                yield
                act.wait_ge(S["f_hlin_ps"], b + 1)
                for t in range(T):
                    last = act.activation(hsa[:, t, :], bank[3][:, t * D:(t + 1) * D], ACT.Copy,
                                          scale=ra[:, 2 + t:3 + t])
                last.then_inc(S["f_hs"], 1)
                yield
                act.wait_ge(S["f_x1nT_ps"], b + 1)
                if after(b, 0):
                    act.wait_ge(S["f_qp_ps"], b * 4)
                if after(b, 0):
                    act.wait_ge(S["f_mid"], b)
                copy(x1Ta[:, :], bank[2][:, 0:N]).then_inc(S["f_x1nT"], 1)
                for c in range(4):
                    yield
                    act.wait_ge(S["f_qp_ps"], b * 4 + (c + 1))
                    if c == 0:
                        if after(b, 0):
                            act.wait_ge(S["f_sim_ps"], b * 4)
                    copy(qp[:, 2 * c:2 * c + 2, :], v3(bank[2 + c % 2], 2, N)).then_inc(S["f_qp"], 1)
                for t in range(T):
                    for g in range(2):
                        yield
                        act.wait_ge(S["f_sim_ps"], b * 4 + (t * 2 + g + 1))
                        if g == 0:
                            if t or after(b, 0):
                                act.wait_ge(S["f_sim_used"], b * 2 + t)
                        half = sim[:, H * g:H * g + H, :].rearrange("p (r e) k -> p r e k", e=2)
                        copy(half[:, :, 0, :], v3(bank[2], 4, NKEYS))
                        copy(half[:, :, 1, :], v3(bank[3], 4, NKEYS)).then_inc(S["f_sim"], 1)
                    yield
                    act.wait_ge(S["f_fs"], b * 2 + (t + 1))
                    act.activation(fv[:, :, :], fv[:, :, :], ACT.Exp).then_inc(S["f_exp"], 1)

            def back(b):
                for c in range(4):
                    yield
                    act.wait_ge(S["c_qT_ps"], b * 4 + (c + 1))
                    if c == 0:
                        if after(b, 0):
                            act.wait_ge(S["c_out_ps"], b)
                    copy(qT[:, 2 * c:2 * c + 2, :], v3([pm, pn][c % 2], 2, N)).then_inc(S["c_qT"], 1)
                for g in range(4):
                    yield
                    act.wait_ge(S["c_kT_ps"], b * 4 + (g + 1))
                    if g or after(b, 0):
                        act.wait_ge(S["c_sim_ps"], b * 4 + g)
                    copy(kT[:, :, :], v3(pk, 2, N)).then_inc(S["c_kT"], 1)
                    yield
                    act.wait_ge(S["c_sm"], b * 4 + (g + 1))
                    for u in range(2):
                        act.activation(sm[:, u, 0, :], sm[:, u, 0, :], ACT.Exp, scale=SCALE,
                                       bias=mxc[:, 2 * u:2 * u + 1], accum_out=rsc[:, 2 * u:2 * u + 1])
                        last = act.activation(sm[:, u, 1:3, :], sm[:, u, 1:3, :], ACT.Exp, scale=SCALE,
                                              bias=mxc[:, 2 * u + 1:2 * u + 2],
                                              accum_out=rsc[:, 2 * u + 1:2 * u + 2])
                    last.then_inc(S["c_exp"], 1)
                    yield
                    act.wait_ge(S["c_pT_ps"], b * 4 + (g + 1))
                    if g or after(b, 0):
                        act.wait_ge(S["c_oT_ps"], b * 4 + g)
                    copy(pT[:, :, :, :].rearrange("p u a b -> p u (a b)"), pmn[:, :, 0:3 * P]).then_inc(S["c_pT"], 1)
                yield
                act.wait_ge(S["c_xn2T_ps"], b + 1)
                if after(b, 0):
                    act.wait_ge(S["c_log_ps"], b)
                copy(xnTc[:, :], pk[:, 0:N]).then_inc(S["c_xn2T"], 1)
                yield
                act.wait_ge(S["c_adjT_ps"], b + 1)
                copy(ATc[:, :, :], v3(pk, T, N)).then_inc(S["c_adjT"], 1)
                yield
                act.wait_ge(S["c_proj_ps"], b + 1)
                for t in range(T):
                    last = act.activation(fh[:, t, :], pmn[:, t, 0:D], ACT.Copy, scale=rc[:, 2 + t:3 + t])
                last.then_inc(S["c_fh"], 1)
                act.activation(gate[:, :, :], pmn[:, :, 2 * D:3 * D], ACT.Exp, scale=-1.0).then_inc(S["c_eg"], 1)
                copy(het[:, :, :], pmn[:, :, D:2 * D]).then_inc(S["c_het"], 1)
                yield
                act.wait_ge(S["c_neg"], b + 1)
                act.activation(g2[:, :, :], g2[:, :, :], ACT.Exp).then_inc(S["c_elu"], 1)
                yield
                act.wait_ge(S["c_xn3T_ps"], b + 1)
                copy(xnTc[:, :], pk[:, 0:N]).then_inc(S["c_xn3T"], 1)
                yield
                act.wait_ge(S["c_sm3"], b + 1)
                act.activation(sw[:, :, :, :], sw[:, :, :, :], ACT.Exp).then_inc(S["c_swe"], 1)
                yield
                act.wait_ge(S["c_uT_ps"], b + 1)
                copy(uT[:, :, :], v3(pn, KC, G)).then_inc(S["c_uT"], 1)
                for c in range(2):
                    yield
                    act.wait_ge(S["c_swT_ps"], b * 2 + (c + 1))
                    copy(swT[:, 2 * c:2 * c + 2, :], v3([pk, pm][c], 2, N)).then_inc(S["c_swT"], 1)
                yield
                act.wait_ge(S["c_inp_ps"], b + 1)
                copy(xp[:, 0:KC, 2:], v3(pk, 2 * KC, G)[:, KC:, :])
                copy(xp[0:HD, KC:KC + 2, 2:], v3(pm, 2, G)[0:HD, :, :])
                copy(yz[:, KC + 2:, :], v3(pk, KC, G)).then_inc(S["c_xp"], 1)
                yield
                act.wait_ge(S["c_dtn"], b + 1)
                act.activation(dte[:, :], dte[:, :], ACT.Exp).then_inc(S["c_dte"], 1)
                yield
                act.wait_ge(S["c_conv"], b + 1)
                act.activation(ez[:, :, :], yz[:, :, :], ACT.Exp, scale=-1.0).then_inc(S["c_cexp"], 1)
                yield
                act.wait_ge(S["c_xc"], b + 1)
                copy(xcd[:, :, 0, :], yz[:, 0:KC, :])
                copy(xcd[:, :, 1, :], yz[:, 0:KC, :])
                copy(bd[:, 0, :], yz[0:HD, KC, :])
                copy(bd[:, 1, :], yz[0:HD, KC, :]).then_inc(S["c_xcd"], 1)
                yield
                act.wait_ge(S["c_seg_ps"], b + 1)
                act.activation(E[:, :, :], v3(pn, H, G), ACT.Exp).then_inc(S["c_E"], 1)
                yield
                act.wait_ge(S["c_xN_ps"], b + 1)
                copy(xN[:, :], pk).then_inc(S["c_xN"], 1)
                yield
                act.wait_ge(S["c_ot_ps"], b + 1)
                copy(otT[:, :, :], v3(pk, KC, G)).then_inc(S["c_ot"], 1)
                yield
                act.wait_ge(S["c_v_ps"], b + 1)
                copy(vv[:, :, :], v3(pm, KC, D)).then_inc(S["c_vv"], 1)

            run_batches(act, FIRST_ACT, ORDER_ACT, LAST_ACT, setup, front, gather, back)

        @block.tensor
        def _(pe):
            def mm(out_, lhsT, rhs, start=True, stop=True):
                return pe.matmul(out_, lhsT, rhs, start=start, stop=stop)

            pe.wait_ge(S["w_front"], 16 * NFRONT)
            pe.wait_ge(S["s_pool"], NPOOL)

            def setup():
                pe.wait_ge(S["w_loaded"], 16 * NLOADS)
                for h in range(H):
                    q = slice((h % 2) * HD, (h % 2) * HD + HD)
                    mm([pk, pm][h % 2][:, (h // 2) * G:(h // 2 + 1) * G], oT[q, h // 2, 0:D], sxn[q, 0:G])
                for h in range(H):
                    q = slice((h % 2) * HD, (h % 2) * HD + HD)
                    c = (H // 2 + h // 2) * G
                    last = mm([pk, pm][h % 2][0:1, c:c + G], sxn[q, G + h // 2:G + h // 2 + 1], sxn[q, 0:G])
                last.then_inc(S["s_pe"], 1)
                pe.wait_ge(S["s_dve_w"], 1)

            def gather(b):
                for n in range(CH * PARTS):
                    j = n // PARTS
                    value = b * CH + (j - 1)
                    if n % PARTS == 0 and not (isinstance(value, int) and value <= 0):
                        pe.wait_ge(S["chunk_saved"], value)
                    pe.wait_ge(S["part_scaled"], b * (PARTS * CH) + (n + 1))
                    for k in range(KP):
                        last = mm(bank[j % 2][:, 0:ROW], ident[:, :], ring[:, n % RING, k, :],
                                  n % PARTS == 0 and k == 0, n % PARTS == PARTS - 1 and k == KP - 1)
                    last.then_inc(S["part_added"], 1)
                    yield

            def front(b):
                pe.wait_ge(S["f_xn"], b + 1)
                if after(b, 0):
                    pe.wait_ge(S["f_sim"], b * 4)
                for t in range(T):
                    last = pe.transpose(bank[2][:, t * P:(t + 1) * P], xna[:, t, :], ident[:, :])
                last.then_inc(S["f_xnT_ps"], 1)
                for t in range(T):
                    for m in range(T):
                        last = pe.transpose(bank[4][:, m * N + t * P:m * N + (t + 1) * P],
                                            adja[:, t, m * P:(m + 1) * P], ident[:, :])
                last.then_inc(S["f_adjT_ps"], 1)
                yield
                pe.wait_ge(S["f_xnT"], b + 1)
                for t in range(T):
                    mm(bank[3][:, t * D:(t + 1) * D], xnTa[:, t * P:(t + 1) * P], w0T_s[:, :], True, False)
                    last = mm(bank[3][:, t * D:(t + 1) * D], ones[64:65, :], b0_r, False, True)
                last.then_inc(S["f_hlin_ps"], 1)
                yield
                pe.wait_ge(S["f_hs"], b + 1)
                pe.wait_ge(S["f_adjT"], b + 1)
                for t in range(T):
                    o = bank[3][:, t * D:(t + 1) * D]
                    for m in range(T):
                        mm(o, ATa[:, m, t * P:(t + 1) * P], hsa[:, m, :], m == 0, False)
                    last = mm(o, ident[:, :], hsa[:, t, :], False, True)
                last.then_inc(S["f_agg_ps"], 1)
                yield
                pe.wait_ge(S["f_x1n"], b + 1)
                for t in range(T):
                    last = pe.transpose(bank[2][:, t * P:(t + 1) * P], xna[:, t, :], ident[:, :])
                last.then_inc(S["f_x1nT_ps"], 1)
                yield
                pe.wait_ge(S["f_x1nT"], b + 1)
                for c in range(4):
                    if c >= 2:
                        yield
                        pe.wait_ge(S["f_qp"], b * 4 + (c - 1))
                    for e in range(2):
                        n = 2 * c + e
                        last = mm(bank[2 + c % 2][:, e * N:(e + 1) * N], wqpk_s[:, n * P:(n + 1) * P], x1Ta[:, :])
                    last.then_inc(S["f_qp_ps"], 1)
                for t in range(T):
                    if t == 0:
                        pe.wait_ge(S["f_qp"], b * 4 + 4)
                    for g in range(2):
                        yield
                        if t + g:
                            pe.wait_ge(S["f_sim"], b * 4 + (t * 2 + g))
                        for e in range(H):
                            r = H * g + e
                            q = slice((r % 2) * HD, (r % 2) * HD + HD)
                            last = mm(bank[2 + e % 2][:, (e // 2) * NKEYS:(e // 2 + 1) * NKEYS],
                                      qp[q, r // 2, t * P:(t + 1) * P], keys_s[q, r // 2, :])
                        last.then_inc(S["f_sim_ps"], 1)

            def back(b):
                pe.wait_ge(S["c_snap"], b + 1)
                for c in range(4):
                    if c >= 2:
                        yield
                        pe.wait_ge(S["c_qT"], b * 4 + (c - 1))
                    for e in range(2):
                        h = 2 * c + e
                        last = mm([pm, pn][c % 2][:, e * N:(e + 1) * N], wq_s[:, h * D:(h + 1) * D], x1Tc[:, :])
                    last.then_inc(S["c_qT_ps"], 1)
                for g in range(4):
                    yield
                    if g or after(b, 0):
                        pe.wait_ge(S["c_oT"], b * 4 + g)
                    for e in range(2):
                        for t in range(T):
                            last = pe.transpose(pk[:, e * N + t * P:e * N + (t + 1) * P],
                                                kv_c[:, t, 2 * g + e, 0:D], ident[:, :])
                    last.then_inc(S["c_kT_ps"], 1)
                    yield
                    pe.wait_ge(S["c_kT"], b * 4 + (g + 1))
                    if g == 0:
                        pe.wait_ge(S["c_qT"], b * 4 + 4)
                    if g or after(b, 0):
                        pe.wait_ge(S["c_pT"], b * 4 + g)
                    for e in range(2):
                        h = 2 * g + e
                        mm(pmn[:, e, 0:P], qT[:, h, 0:P], kT[:, e, 0:P])
                        last = mm(pmn[:, e, P:3 * P], qT[:, h, P:2 * P], kT[:, e, :])
                    last.then_inc(S["c_sim_ps"], 1)
                    yield
                    pe.wait_ge(S["c_prob"], b * 4 + (g + 1))
                    for e in range(2):
                        for s in range(3):
                            last = pe.transpose(pmn[:, e, s * P:(s + 1) * P], sm[:, e, s, :], ident[:, :])
                    last.then_inc(S["c_pT_ps"], 1)
                    yield
                    pe.wait_ge(S["c_pT"], b * 4 + (g + 1))
                    for e in range(2):
                        h = 2 * g + e
                        o = pk[:, e * N:(e + 1) * N]
                        mm(o[:, 0:P], kv_c[:, 0, h, D:], pT[:, e, 0, :])
                        mm(o[:, P:], kv_c[:, 0, h, D:], pT[:, e, 1, :], True, False)
                        last = mm(o[:, P:], kv_c[:, 1, h, D:], pT[:, e, 2, :], False, True)
                    last.then_inc(S["c_oT_ps"], 1)
                yield
                pe.wait_ge(S["c_oT"], b * 4 + 4)
                for t in range(T):
                    for h in range(H):
                        last = mm(pk[:, t * D:(t + 1) * D], oT[:, h, t * P:(t + 1) * P], wo_s[:, h, :],
                                  h == 0, h == H - 1)
                last.then_inc(S["c_wo_ps"], 1)
                yield
                pe.wait_ge(S["c_xn2"], b + 1)
                for t in range(T):
                    last = pe.transpose(pk[:, t * P:(t + 1) * P], xnc[:, t, :], ident[:, :])
                last.then_inc(S["c_xn2T_ps"], 1)
                yield
                pe.wait_ge(S["c_xn2T"], b + 1)
                for t in range(T):
                    for m in range(T):
                        last = pe.transpose(pk[:, m * N + t * P:m * N + (t + 1) * P],
                                            adjc[:, t, m * P:(m + 1) * P], ident[:, :])
                last.then_inc(S["c_adjT_ps"], 1)
                for t in range(T):
                    mm(pmn[:, t, 0:3 * D], xnTc[:, t * P:(t + 1) * P], w1_s[:, :], True, False)
                    last = mm(pmn[:, t, 2 * D:3 * D], ones[64:65, :], bt_r, False, True)
                last.then_inc(S["c_proj_ps"], 1)
                yield
                pe.wait_ge(S["c_fh"], b + 1)
                pe.wait_ge(S["c_adjT"], b + 1)
                for t in range(T):
                    for m in range(T):
                        last = mm(pk[:, t * D:(t + 1) * D], ATc[:, m, t * P:(t + 1) * P], fh[:, m, :],
                                  m == 0, m == T - 1)
                last.then_inc(S["c_hom_ps"], 1)
                yield
                pe.wait_ge(S["c_xn3"], b + 1)
                for t in range(T):
                    last = pe.transpose(pk[:, t * P:(t + 1) * P], xnc[:, t, :], ident[:, :])
                last.then_inc(S["c_xn3T_ps"], 1)
                yield
                pe.wait_ge(S["c_xn3T"], b + 1)
                pe.wait_ge(S["c_het"], b + 1)
                for t in range(T):
                    mm(pmn[:, t, :], xnTc[:, t * P:(t + 1) * P], ws_s[:, :], True, False)
                    last = mm(pmn[:, t, :], ones[0:1, :], sl_r, False, True)
                last.then_inc(S["c_log_ps"], 1)
                yield
                pe.wait_ge(S["c_sw"], b + 1)
                sws = sw[:, :, :, :].rearrange("p t h g -> p t (h g)")
                for t in range(T):
                    mm(pk, xnc[:, t, :], sws[:, t, :], t == 0, t == T - 1)
                for t in range(T):
                    last = mm(pm, ones[:, :], sws[:, t, :], t == 0, t == T - 1)
                last.then_inc(S["c_sx_ps"], 1)
                yield
                pe.wait_ge(S["c_sxn"], b + 1)
                for h in range(H):
                    q = slice((h % 2) * HD, (h % 2) * HD + HD)
                    o = pn[q, (h // 2) * G:(h // 2 + 1) * G]
                    c = slice(h * HD, (h + 1) * HD)
                    mm(o, wfx_s[:, c], sxn[:, c], True, False)
                    last = mm(o, bfx_r[:, c], sfr[32:33, c], False, True)
                last.then_inc(S["c_uT_ps"], 1)
                for c in range(2):
                    for e in range(2):
                        for t in range(T):
                            n = 2 * c + e
                            last = pe.transpose([pk, pm][c][:, e * N + t * P:e * N + (t + 1) * P],
                                                sws[:, t, n * P:(n + 1) * P], ident[:, :])
                    last.then_inc(S["c_swT_ps"], 1)
                yield
                pe.wait_ge(S["c_uT"], b + 1)
                pe.wait_ge(S["c_swT"], b * 2 + 2)
                for m in range(2 * KC):
                    for k in range(KC):
                        mm(pk[:, m * G:(m + 1) * G], in_s[:, k, m * P:(m + 1) * P], uT[:, k, :], k == 0, k == KC - 1)
                for m in range(2):
                    c = 2 * DI + m * HD
                    for k in range(KC):
                        mm(pm[0:HD, m * G:(m + 1) * G], in_s[:, k, c:c + HD], uT[:, k, :], k == 0, k == KC - 1)
                for m in range(2):
                    c = 2 * DI + 2 * HD + m * H
                    for k in range(KC):
                        last = mm(pm[m * G:(m + 1) * G, 2 * G:2 * G + H], uT[:, k, :], in_s[:, k, c:c + H],
                                  k == 0, k == KC - 1)
                last.then_inc(S["c_inp_ps"], 1)
                yield
                pe.wait_ge(S["c_rda"], b + 1)
                mm(pn, segL[:, :], rda[:, :, :].rearrange("p a b -> p (a b)")).then_inc(S["c_seg_ps"], 1)
                yield
                pe.wait_ge(S["c_xcd"], b + 1)
                for c in range(KC):
                    last = pe.transpose(pk[:, c * P:(c + 1) * P], xcd[:, c, :, :].rearrange("p a b -> p (a b)"), ident[:, :])
                last.then_inc(S["c_xN_ps"], 1)
                mm(pm[:, 0:G], bd[:, :, :].rearrange("p a b -> p (a b)"),
                   yz[0:HD, KC + 1, :]).then_inc(S["c_cb_ps"], 1)
                yield
                pe.wait_ge(S["c_xN"], b + 1)
                pe.wait_ge(S["c_M"], b + 1)
                for h in range(H):
                    q = slice((h % 2) * HD, (h % 2) * HD + HD)
                    mm(pk[q, (h // 2) * G:(h // 2 + 1) * G], xN[:, h * HD:(h + 1) * HD], Mp[:, h, 1:G + 1])
                for m in range(KC):
                    for k in range(KC):
                        last = mm(pk[:, (KC + m) * G:(KC + m + 1) * G], fcd_s[:, k, m * P:(m + 1) * P], yz[:, k, :],
                                  k == 0, k == KC - 1)
                last.then_inc(S["c_y_ps"], 1)
                yield
                pe.wait_ge(S["c_sq"], b + 1)
                for k in range(KC):
                    last = mm(pm[:, 0:G], ones[:, :], sq[:, k, :], k == 0, k == KC - 1)
                last.then_inc(S["c_ms_ps"], 1)
                yield
                pe.wait_ge(S["c_yn"], b + 1)
                for m in range(KC):
                    for k in range(KC):
                        last = mm(pk[:, m * G:(m + 1) * G], hout_s[:, k, m * P:(m + 1) * P], yg[:, k, :],
                                  k == 0, k == KC - 1)
                last.then_inc(S["c_ot_ps"], 1)
                yield
                pe.wait_ge(S["c_ot"], b + 1)
                pe.sem_inc(S["pe_turn"], 1)
                for h in range(H):
                    q = slice((h % 2) * HD, (h % 2) * HD + HD)
                    last = mm(pm[q, (h // 2) * D:(h // 2 + 1) * D], otT[q, h // 2, :], out_s[q, h // 2, :])
                last.then_inc(S["c_v_ps"], 1)
                yield
                pe.wait_ge(S["c_vv"], b + 1)
                for t in range(T):
                    o = pn[:, t * D:(t + 1) * D]
                    for c in range(KC):
                        mm(o, swT[:, c, t * P:(t + 1) * P], vv[:, c, :], c == 0, False)
                    last = mm(o, ones[64:65, :], ob_r, False, True)
                last.then_inc(S["c_out_ps"], 1)

            run_batches(pe, FIRST_PE, ORDER_PE, LAST_PE, setup, front, gather, back)

        @block.vector
        def _(dve):
            def bc(ap, n):
                return ap.unsqueeze(2).to_broadcast([ap.shape[0], ap.shape[1], n])

            def bm(ap, n):
                return ap.unsqueeze(1).to_broadcast([ap.shape[0], n, ap.shape[1]])

            tt, ts, stt, copy = dve.tensor_tensor, dve.tensor_scalar, dve.scalar_tensor_tensor, dve.tensor_copy

            def rsqrt(dst, src, tmp):
                dve.wait_ge(S["dve_step"], steps())
                ts(dst.bitcast(i32), src.bitcast(i32), 1, None,
                   ALU.logical_shift_right).then_inc(S["dve_step"], step())
                ts(src, src, -0.5, None, ALU.mult).then_inc(S["dve_step"], step())
                dve.wait_ge(S["dve_step"], steps())
                ts(dst.bitcast(i32), dst.bitcast(i32), -1.0, 1597463007.0, ALU.mult,
                   ALU.add).then_inc(S["dve_step"], step())
                for _ in range(3):
                    dve.wait_ge(S["dve_step"], steps())
                    tt(tmp, dst, dst, ALU.mult).then_inc(S["dve_step"], step())
                    dve.wait_ge(S["dve_step"], steps())
                    tt(tmp, tmp, src, ALU.mult).then_inc(S["dve_step"], step())
                    dve.wait_ge(S["dve_step"], steps())
                    stt(dst, tmp, 1.5, dst, ALU.add, ALU.mult).then_inc(S["dve_step"], step())
                dve.wait_ge(S["dve_step"], steps())

            def stats(src, st, mv):
                for t in range(T):
                    dve.bn_stats(st[:, t, :], src[:, t, :]).then_inc(S["dve_step"], step())
                dve.wait_ge(S["dve_step"], steps())
                for t in range(T):
                    dve.bn_aggr(mv[:, t, :], st[:, t, :]).then_inc(S["dve_step"], step())
                dve.wait_ge(S["dve_step"], steps())

            def normalise(dst, src, mv, r, signal):
                for t in range(T):
                    last = ts(dst[:, t, :], src[:, t, :], mv[:, t, 0:1], r[:, t:t + 1], ALU.subtract, ALU.mult)
                last.then_inc(signal, 1)

            dve.wait_ge(S["s_pool"], NPOOL)
            ts(hoff[:, :], hoff[:, :], 16.0, None, ALU.mult).then_inc(S["dve_step"], step())

            def odd_even(ap, e):
                return ap.rearrange("p (h e g) -> p h e g", e=2, g=G)[:, :, e, :]

            def setup():
                dve.wait_ge(S["w_loaded"], 16 * NLOADS)
                ts(roota[:, :], roota[:, :], 0.5, None, ALU.mult).then_inc(S["dve_step"], step())
                dve.wait_ge(S["dve_step"], steps())
                ts(roota[:, :], roota[:, :], 78.0, None, ALU.min).then_inc(S["s_dve_a"], 1)
                ts(rtemp[:, :], rtemp[:, :], 1e-6, None, ALU.max).then_inc(S["dve_step"], step())
                for k in range(KC):
                    ts(hout_s[:, k, :], hout_s[:, k, :], nw_s[:, k:k + 1], None,
                       ALU.mult).then_inc(S["dve_step"], step())
                dve.wait_ge(S["dve_step"], steps())
                dve.reciprocal(rtemp[:, :], rtemp[:, :]).then_inc(S["dve_step"], step())
                dve.wait_ge(S["dve_step"], steps())
                dve.wait_ge(S["s_pe"], 1)
                for e in range(2):
                    product = v3([pk, pm][e], H, G)
                    tt(odd_even(ws_s[:, :], e), product[:, 0:H // 2, :],
                       bc(rtemp[:, :].rearrange("p (h e) -> p h e", e=2)[:, :, e], G),
                       ALU.mult).then_inc(S["dve_step"], step())
                    tt(odd_even(sl_r, e), product[0:1, H // 2:, :], bm(oT[0:1, 4, 0:G], H // 2),
                       ALU.add).then_inc(S["dve_step"], step())
                dve.wait_ge(S["dve_step"], steps())
                dve.wait_ge(S["s_act"], 1)
                tt(v3(sl_r, H, G), v3(sl_r, H, G), bc(rtemp[0:1, :], G), ALU.mult).then_inc(S["s_dve_w"], 1)
                dve.wait_ge(S["s_dve_w"], 1)

            def opening(i, has_back):
                if has_back:
                    if after(i, 1):
                        dve.wait_ge(S["c_out_ps"], i - 1)
                    copy(x1c[:, :, :], x1m[:, :, :]).then_inc(S["dve_step"], step())
                    copy(x1Tc[:, :], x1Tm[:, :]).then_inc(S["dve_step"], step())
                    dve.wait_ge(S["dve_step"], steps())
                if isinstance(i, int) and i == NB:
                    return
                copy(x1m[:, :, :], x1a[:, :, :]).then_inc(S["dve_step"], step())
                dve.wait_ge(S["f_x1nT"], i + 1)
                copy(x1Tm[:, :], x1Ta[:, :]).then_inc(S["f_mid"], 1)
                dve.wait_ge(S["f_mid"], i + 1)

            def handover(b):
                for t in range(T):
                    dve.wait_ge(S["f_sim_used"], b * 2 + (t + 1))
                    dve.wait_ge(S["f_weights"], b * 2 + (t + 1))
                    if not (isinstance(b, int) and b == 0):
                        dve.wait_ge(S["part_scaled"], b * (PARTS * CH) + ((t + 1) * H * PARTS - PARTS * CH))
                    copy(w_cur[:, t, :], w_next[:, t, :]).then_inc(S["dve_step"], step())
                    copy(idx_cur[:, t, :], idx_next[:, t, :]).then_inc(S["idx_ready"], 1)
                    yield

            def gather(b):
                for j in range(CH):
                    t, h = divmod(j, H)
                    dve.wait_ge(S["part_added"], b * (PARTS * CH) + (PARTS * (j + 1)))
                    copy(kv_acc[:, t, h, :], bank[j % 2][:, 0:ROW]).then_inc(S["chunk_saved"], 1)
                    yield

            def front(b):
                dve.wait_ge(S["f_loaded"], b * 48 + 48)
                dve.wait_ge(S["dve_step"], steps())
                stats(xa, sta, mva)
                dve.tensor_reduce(out=va[:, 2:4], in_=adja[:, :, :], axis=X,
                                  op=ALU.add).then_inc(S["dve_step"], step())
                ts(va[:, 0:2], mva[:, :, 1], 1e-5, None, ALU.add).then_inc(S["dve_step"], step())
                dve.wait_ge(S["dve_step"], steps())
                ts(va[:, 2:4], va[:, 2:4], 1.0, 1e-8, ALU.add, ALU.add).then_inc(S["dve_step"], step())
                yield
                if after(b, 0):
                    dve.wait_ge(S["f_hs"], b)
                rsqrt(ra[:, :], va[:, :], rta[:, :])
                yield
                if after(b, 0):
                    dve.wait_ge(S["f_x1nT_ps"], b)
                normalise(xna, xa, mva, ra, S["f_xn"])
                yield
                dve.wait_ge(S["f_agg_ps"], b + 1)
                for t in range(T):
                    ts(x1a[:, t, :], bank[3][:, t * D:(t + 1) * D], ra[:, 2 + t:3 + t], mska[:, t:t + 1],
                            ALU.mult, ALU.mult).then_inc(S["dve_step"], step())
                dve.wait_ge(S["dve_step"], steps())
                stt(x1a[:, :, :], x1a[:, :, :], 0.0, xa[:, :, :], ALU.max, ALU.add).then_inc(S["f_x1"], 1)
                yield
                dve.wait_ge(S["f_x1"], b + 1)
                stats(x1a, sta, mva)
                ts(va[:, 0:2], mva[:, :, 1], 1e-5, None, ALU.add).then_inc(S["dve_step"], step())
                rsqrt(ra[:, 0:2], va[:, 0:2], rta[:, 0:2])
                normalise(xna, x1a, mva, ra, S["f_x1n"])
                for t in range(T):
                    for half in range(2):
                        group = range(H * half, H * half + H)
                        yield
                        dve.wait_ge(S["f_sim"], b * 4 + (t * 2 + half + 1))
                        dve.sem_inc(S["dve_turn"], 1)
                        for r in group:
                            dve.max(tv[:, r, 0:8], sim[:, r, :]).then_inc(S["dve_step"], step())
                        dve.wait_ge(S["dve_step"], steps())
                        for r in group:
                            if r % 4 == 0:
                                yield
                            dve.max_index(ti[:, r, 0:8], tv[:, r, 0:8], sim[:, r, :]).then_inc(S["dve_step"], step())
                            dve.match_replace(sim[:, r, :], tv[:, r, 0:8], sim[:, r, :],
                                              LOWEST).then_inc(S["dve_step"], step())
                        dve.wait_ge(S["dve_step"], steps())
                        yield
                        for r in group:
                            dve.max(tv[:, r, 8:16], sim[:, r, :]).then_inc(S["dve_step"], step())
                        dve.wait_ge(S["dve_step"], steps())
                        yield
                        for r in group:
                            dve.max_index(ti[:, r, 8:16], tv[:, r, 8:16],
                                          sim[:, r, :]).then_inc(S["dve_step"], step())
                        dve.wait_ge(S["dve_step"], steps())
                    yield
                    copy(tf[:, :, :], ti[:, :, :]).then_inc(S["dve_step"], step())
                    dve.wait_ge(S["dve_step"], steps())
                    ts(tf[:, H:, :], tf[:, H:, :], float(NKEYS), None, ALU.mult).then_inc(S["dve_step"], step())
                    tt(tf[:, 0:H, :], tf[:, 0:H, :], bc(hoff[:, :], K), ALU.add).then_inc(S["dve_step"], step())
                    dve.wait_ge(S["dve_step"], steps())
                    for dst, src in ((cand, tv), (cidx, tf)):
                        a, c = src[:, 0:H, :], src[:, H:, :]
                        for i in range(K):
                            w = WIDTH[i]
                            if w > 1:
                                tt(dst[:, :, START[i]:START[i] + w], a[:, :, i:i + 1].to_broadcast([P, H, w]),
                                        c[:, :, 0:w], ALU.add).then_inc(S["dve_step"], step())
                        i = WIDTH.index(1)
                        tt(dst[:, :, START[i]:], a[:, :, i:], c[:, :, 0:1].to_broadcast([P, H, K - i]),
                           ALU.add).then_inc(S["dve_step"], step())
                    dve.wait_ge(S["dve_step"], steps())
                    yield
                    for h in range(H):
                        dve.max(fv[:, h, 0:8], cand[:, h, :]).then_inc(S["dve_step"], step())
                    dve.wait_ge(S["dve_step"], steps())
                    for h in range(H):
                        dve.max_index(fp[:, h, 0:8], fv[:, h, 0:8], cand[:, h, :]).then_inc(S["dve_step"], step())
                        dve.match_replace(cand[:, h, :], fv[:, h, 0:8], cand[:, h, :],
                                          LOWEST).then_inc(S["dve_step"], step())
                    dve.wait_ge(S["dve_step"], steps())
                    yield
                    for h in range(H):
                        dve.max(fv[:, h, 8:16], cand[:, h, :]).then_inc(S["dve_step"], step())
                    dve.wait_ge(S["dve_step"], steps())
                    for h in range(H):
                        dve.max_index(fp[:, h, 8:16], fv[:, h, 8:16], cand[:, h, :]).then_inc(S["dve_step"], step())
                    dve.wait_ge(S["dve_step"], steps())
                    copy(fpf[:, :, :], fp[:, :, :]).then_inc(S["dve_step"], step())
                    copy(fs[:, :], fv[:, :, 0]).then_inc(S["dve_step"], step())
                    dve.wait_ge(S["dve_step"], steps())
                    tt(fv[:, :, :], fv[:, :, :], bc(fs[:, :], K), ALU.subtract).then_inc(S["f_fs"], 1)
                    for h in range(H):
                        yield
                        tt(hot[:, :, :], bc(fpf[:, h, :], NC), bm(iota[:, :], K),
                           ALU.is_equal).then_inc(S["dve_step"], step())
                        dve.wait_ge(S["dve_step"], steps())
                        tt(hot[:, :, :], hot[:, :, :], bm(cidx[:, h, :], K), ALU.mult).then_inc(S["dve_step"], step())
                        dve.wait_ge(S["dve_step"], steps())
                        dve.tensor_reduce(out=fidx[:, h, :], in_=hot[:, :, :], axis=X,
                                          op=ALU.add).then_inc(S["dve_step"], step())
                        dve.wait_ge(S["dve_step"], steps())
                    copy(idx_next[:, t, :], fidx[:, :, :].rearrange("p a b -> p (a b)")).then_inc(S["f_sim_used"], 1)
                    yield
                    dve.wait_ge(S["f_exp"], b * 2 + (t + 1))
                    dve.tensor_reduce(out=fs[:, :], in_=fv[:, :, :], axis=X,
                                      op=ALU.add).then_inc(S["dve_step"], step())
                    dve.wait_ge(S["dve_step"], steps())
                    dve.reciprocal(fs[:, :], fs[:, :]).then_inc(S["dve_step"], step())
                    dve.wait_ge(S["dve_step"], steps())
                    tt(w_next[:, t, :].rearrange("p (a b) -> p a b", b=K), fv[:, :, :],
                       bc(fs[:, :], K), ALU.mult).then_inc(S["f_weights"], 1)

            def back(b):
                dve.wait_ge(S["chunk_saved"], b * CH + CH)
                dve.wait_ge(S["dve_step"], steps())
                copy(kv_c[:, :, :, :], kv_acc[:, :, :, :]).then_inc(S["c_snap"], 1)
                for g in range(4):
                    yield
                    dve.wait_ge(S["c_sim_ps"], b * 4 + (g + 1))
                    for e in range(2):
                        tt(sm[:, e, :, :], v3(pmn[:, e, :], 3, P), causal[:, :, :],
                           ALU.add).then_inc(S["dve_step"], step())
                    dve.wait_ge(S["dve_step"], steps())
                    for e in range(2):
                        dve.tensor_reduce(out=mxc[:, 2 * e:2 * e + 1], in_=sm[:, e, 0, :], axis=X,
                                          op=ALU.max).then_inc(S["dve_step"], step())
                        dve.tensor_reduce(out=mxc[:, 2 * e + 1:2 * e + 2],
                                               in_=sm[:, e, 1:3, :].rearrange("p a b -> p (a b)"), axis=X,
 op=ALU.max).then_inc(S["dve_step"], step())
                    dve.wait_ge(S["dve_step"], steps())
                    ts(mxc[:, :], mxc[:, :], -SCALE, None, ALU.mult).then_inc(S["c_sm"], 1)
                    yield
                    dve.wait_ge(S["c_exp"], b * 4 + (g + 1))
                    dve.reciprocal(rsc[:, :], rsc[:, :]).then_inc(S["dve_step"], step())
                    dve.wait_ge(S["dve_step"], steps())
                    for e in range(2):
                        ts(sm[:, e, 0, :], sm[:, e, 0, :], rsc[:, 2 * e:2 * e + 1], None, ALU.mult)
                        last = ts(sm[:, e, 1:3, :], sm[:, e, 1:3, :], rsc[:, 2 * e + 1:2 * e + 2], None, ALU.mult)
                    last.then_inc(S["c_prob"], 1)
                    yield
                    dve.wait_ge(S["c_oT_ps"], b * 4 + (g + 1))
                    copy(oT[:, 2 * g:2 * g + 2, :], v3(pk, 2, N)).then_inc(S["c_oT"], 1)
                yield
                dve.wait_ge(S["c_wo_ps"], b + 1)
                tt(x2[:, :, :], v3(pk, T, D), x1c[:, :, :], ALU.add).then_inc(S["c_x2"], 1)
                yield
                dve.wait_ge(S["c_adj"], b * 16 + 16)
                dve.wait_ge(S["c_x2"], b + 1)
                for t in range(T):
                    stt(absj[:, :], adjc[:, t, :], -1.0, adjc[:, t, :], ALU.mult, ALU.max,
                             accum_out=vc[:, 2 + t:3 + t]).then_inc(S["dve_step"], step())
                    dve.wait_ge(S["dve_step"], steps())
                stats(x2, stc, mvc)
                ts(vc[:, 0:2], mvc[:, :, 1], 1e-5, None, ALU.add).then_inc(S["dve_step"], step())
                ts(vc[:, 2:4], vc[:, 2:4], 1e-6, None, ALU.add).then_inc(S["dve_step"], step())
                rsqrt(rc[:, 0:4], vc[:, 0:4], rtc[:, 0:4])
                normalise(xnc, x2, mvc, rc, S["c_xn2"])
                yield
                dve.wait_ge(S["c_eg"], b + 1)
                ts(gate[:, :, :], gate[:, :, :], 1.0, None, ALU.add).then_inc(S["dve_step"], step())
                dve.wait_ge(S["dve_step"], steps())
                dve.reciprocal(gate[:, :, :], gate[:, :, :]).then_inc(S["dve_step"], step())
                yield
                dve.wait_ge(S["c_hom_ps"], b + 1)
                dve.wait_ge(S["c_het"], b + 1)
                for t in range(T):
                    stt(g1[:, t, :], pk[:, t * D:(t + 1) * D], rc[:, 2 + t:3 + t], het[:, t, :], ALU.mult,
                        ALU.subtract).then_inc(S["dve_step"], step())
                dve.wait_ge(S["dve_step"], steps())
                tt(g1[:, :, :], g1[:, :, :], gate[:, :, :], ALU.mult).then_inc(S["dve_step"], step())
                dve.wait_ge(S["dve_step"], steps())
                tt(g1[:, :, :], g1[:, :, :], het[:, :, :], ALU.add).then_inc(S["dve_step"], step())
                dve.wait_ge(S["dve_step"], steps())
                ts(g2[:, :, :], g1[:, :, :], 0.0, None, ALU.min).then_inc(S["c_neg"], 1)
                yield
                dve.wait_ge(S["c_elu"], b + 1)
                stt(g1[:, :, :], g1[:, :, :], 0.0, g2[:, :, :], ALU.max, ALU.add).then_inc(S["dve_step"], step())
                dve.wait_ge(S["dve_step"], steps())
                stt(x3[:, :, :], g1[:, :, :], -1.0, x2[:, :, :], ALU.add, ALU.add).then_inc(S["dve_step"], step())
                dve.wait_ge(S["dve_step"], steps())
                stats(x3, stc, mvc)
                ts(vc[:, 0:2], mvc[:, :, 1], 1e-5, None, ALU.add).then_inc(S["dve_step"], step())
                rsqrt(rc[:, 0:2], vc[:, 0:2], rtc[:, 0:2])
                yield
                dve.wait_ge(S["c_xn2T_ps"], b + 1)
                normalise(xnc, x3, mvc, rc, S["c_xn3"])
                yield
                dve.wait_ge(S["c_log_ps"], b + 1)
                logits = pmn.rearrange("p t (h g) -> p t h g", g=G)
                for t in range(T):
                    dve.tensor_reduce(out=smx[:, t * H:(t + 1) * H], in_=logits[:, t], axis=X,
                                      op=ALU.max).then_inc(S["dve_step"], step())
                dve.wait_ge(S["dve_step"], steps())
                for t in range(T):
                    last = tt(sw[:, t, :, :], logits[:, t], bc(smx[:, t * H:(t + 1) * H], G), ALU.subtract)
                last.then_inc(S["c_sm3"], 1)
                yield
                dve.wait_ge(S["c_swe"], b + 1)
                sw2 = sw[:, :, :, :].rearrange("p t h g -> p (t h) g")
                dve.tensor_reduce(out=smx[:, :], in_=sw2, axis=X, op=ALU.add).then_inc(S["dve_step"], step())
                dve.wait_ge(S["dve_step"], steps())
                dve.reciprocal(smx[:, :], smx[:, :]).then_inc(S["dve_step"], step())
                dve.wait_ge(S["dve_step"], steps())
                tt(sw2, sw2, bc(smx[:, :], G), ALU.mult).then_inc(S["c_sw"], 1)
                yield
                dve.wait_ge(S["c_sx_ps"], b + 1)
                ts(srcp[:, :], pm, 1e-5, None, ALU.add).then_inc(S["dve_step"], step())
                dve.wait_ge(S["dve_step"], steps())
                dve.reciprocal(srcp[:, :], srcp[:, :]).then_inc(S["dve_step"], step())
                dve.wait_ge(S["dve_step"], steps())
                tt(sfr[32:33, :], pm[32:33, :], srcp[32:33, :], ALU.mult).then_inc(S["dve_step"], step())
                tt(sxn[:, :], pk, srcp[:, :], ALU.mult).then_inc(S["c_sxn"], 1)
                yield
                dve.wait_ge(S["c_xp"], b + 1)
                tt(dtx[:, :], pm[:, 2 * G:2 * G + H], dtb_s[:, :], ALU.add).then_inc(S["dve_step"], step())
                dve.wait_ge(S["dve_step"], steps())
                stt(dte[:, :], dtx[:, :], -1.0, dtx[:, :], ALU.mult, ALU.min).then_inc(S["c_dtn"], 1)
                taps = [cw[:, :, k:k + 1].to_broadcast([P, KC + 2, G]) for k in range(3)]
                y6 = yz[:, 0:KC + 2, :]
                tt(y6, xp[:, :, 0:G], taps[0], ALU.mult).then_inc(S["dve_step"], step())
                for k in (1, 2):
                    dve.wait_ge(S["dve_step"], steps())
                    tt(ct[:, :, :], xp[:, :, k:k + G], taps[k], ALU.mult).then_inc(S["dve_step"], step())
                    dve.wait_ge(S["dve_step"], steps())
                    tt(y6, y6, ct[:, :, :], ALU.add).then_inc(S["dve_step"], step())
                dve.wait_ge(S["dve_step"], steps())
                tt(y6, y6, bc(cb[:, :], G), ALU.add).then_inc(S["c_conv"], 1)
                yield
                dve.wait_ge(S["c_dte"], b + 1)
                ts(dtz[:, :], dte[:, :], 2.0, None, ALU.add).then_inc(S["dve_step"], step())
                dve.wait_ge(S["dve_step"], steps())
                dve.reciprocal(dtz[:, :], dtz[:, :]).then_inc(S["dve_step"], step())
                dve.wait_ge(S["dve_step"], steps())
                tt(dtz[:, :], dtz[:, :], dte[:, :], ALU.mult).then_inc(S["dve_step"], step())
                dve.wait_ge(S["dve_step"], steps())
                tt(dtq[:, :], dtz[:, :], dtz[:, :], ALU.mult).then_inc(S["dve_step"], step())
                dve.wait_ge(S["dve_step"], steps())
                ts(dtp[:, :], dtq[:, :], 1.0 / 15, None, ALU.mult).then_inc(S["dve_step"], step())
                for n in (13, 11, 9, 7, 5, 3):
                    dve.wait_ge(S["dve_step"], steps())
                    stt(dtp[:, :], dtp[:, :], 1.0 / n, dtq[:, :], ALU.add, ALU.mult).then_inc(S["dve_step"], step())
                dve.wait_ge(S["dve_step"], steps())
                stt(dtp[:, :], dtp[:, :], 1.0, dtz[:, :], ALU.add, ALU.mult).then_inc(S["dve_step"], step())
                dve.wait_ge(S["dve_step"], steps())
                ts(dtz[:, :], dtx[:, :], 0.0, None, ALU.max).then_inc(S["dve_step"], step())
                dve.wait_ge(S["dve_step"], steps())
                stt(dts[:, :], dtp[:, :], 2.0, dtz[:, :], ALU.mult, ALU.add).then_inc(S["dve_step"], step())
                dve.wait_ge(S["dve_step"], steps())
                tt(da[:, :], dts[:, :], roota[:, :], ALU.mult).then_inc(S["dve_step"], step())
                dve.wait_ge(S["dve_step"], steps())
                stt(da[:, :], da[:, :], 1e4, roota[:, :], ALU.min, ALU.mult).then_inc(S["dve_step"], step())
                dve.wait_ge(S["dve_step"], steps())
                ts(da[:, :], da[:, :], -1.0, -120.0, ALU.mult, ALU.max).then_inc(S["dve_step"], step())
                dve.wait_ge(S["dve_step"], steps())
                tt(rda[:, :, :], bc(da[:, :], G), bm(maskR[:, :], H), ALU.mult).then_inc(S["c_rda"], 1)
                yield
                dve.wait_ge(S["c_cexp"], b + 1)
                ts(ez[:, :, :], ez[:, :, :], 1.0, None, ALU.add).then_inc(S["dve_step"], step())
                dve.wait_ge(S["dve_step"], steps())
                dve.reciprocal(ez[:, :, :], ez[:, :, :]).then_inc(S["dve_step"], step())
                dve.wait_ge(S["dve_step"], steps())
                tt(yz[:, :, :], yz[:, :, :], ez[:, :, :], ALU.mult).then_inc(S["c_xc"], 1)
                yield
                dve.wait_ge(S["c_cb_ps"], b + 1)
                tt(cbm[:, :], pm[:, 0:G], maskE[:, :], ALU.mult).then_inc(S["dve_step"], step())
                yield
                dve.wait_ge(S["c_E"], b + 1)
                dve.wait_ge(S["dve_step"], steps())
                tt(E[:, :, :], E[:, :, :], bm(cbm[:, :], H), ALU.mult).then_inc(S["dve_step"], step())
                dve.wait_ge(S["dve_step"], steps())
                tt(Mp[0:G, :, 2:], E[0:G, :, :], bc(dts[0:G, :], G), ALU.mult)
                tt(Mp[G:P, :, 0:G], E[G:P, :, :], bc(dts[G:P, :], G), ALU.mult).then_inc(S["c_M"], 1)
                yield
                dve.wait_ge(S["c_y_ps"], b + 1)
                ys = v3(pk, 2 * KC, G)
                tt(yg[:, :, :], ys[:, KC:, :], bc(drep_s[:, :], G), ALU.add).then_inc(S["dve_step"], step())
                dve.wait_ge(S["dve_step"], steps())
                tt(yg[:, :, :], yg[:, :, :], yz[:, 0:KC, :], ALU.mult).then_inc(S["dve_step"], step())
                dve.wait_ge(S["dve_step"], steps())
                tt(yg[:, :, :], yg[:, :, :], ys[:, 0:KC, :], ALU.add).then_inc(S["dve_step"], step())
                dve.wait_ge(S["dve_step"], steps())
                tt(yg[:, :, :], yg[:, :, :], yz[:, KC + 2:, :], ALU.mult).then_inc(S["dve_step"], step())
                dve.wait_ge(S["dve_step"], steps())
                tt(sq[:, :, :], yg[:, :, :], yg[:, :, :], ALU.mult).then_inc(S["c_sq"], 1)
                yield
                dve.wait_ge(S["c_ms_ps"], b + 1)
                ts(vc[:, :], pm[:, 0:G], 1.0 / DI, 1e-5, ALU.mult, ALU.add).then_inc(S["dve_step"], step())
                rsqrt(rc[:, :], vc[:, :], rtc[:, :])
                tt(yg[:, :, :], yg[:, :, :], bm(rc[:, :], KC), ALU.mult).then_inc(S["c_yn"], 1)
                yield
                dve.wait_ge(S["c_out_ps"], b + 1)
                if after(b, 0):
                    dve.wait_ge(S["stored"], b * 16)
                tt(res[:, :, :], v3(pn, T, D), x3[:, :, :], ALU.add).then_inc(S["c_res"], 1)

            run_batches(dve, FIRST_DVE, ORDER_DVE, LAST_DVE, setup, front, gather, back,
                        opening, handover, lambda: restart(dve))
            dve.wait_ge(S["dve_step"], steps())



_NB, _N, _D = 32, 256, 128


def kernel(x, adj, nodemask, L0_gnn_W, L0_gnn_b, L0_ffn_Wq_pk, L0_ffn_pk_keys, L0_ffn_Wq, L0_ffn_keys_table,
           L0_ffn_values_table, L0_ffn_Wo, L1_gnn_theta, L1_gnn_W_h, L1_gnn_W_t, L1_gnn_b_t, L1_ffn_W_fx,
           L1_ffn_b_fx, L1_ffn_W_x, L1_ffn_b_x, L1_ffn_W_slice, L1_ffn_b_slice, L1_ffn_temperature,
           L1_ffn_hy_in_w, L1_ffn_hy_conv_w, L1_ffn_hy_conv_b, L1_ffn_hy_dt_bias, L1_ffn_hy_A_log,
           L1_ffn_hy_D, L1_ffn_hy_fcD_w, L1_ffn_hy_norm_w, L1_ffn_hy_out_w, L1_ffn_out_w, L1_ffn_out_b):
    import numpy as np
    import concourse.bacc as bacc
    from concourse.bass_utils import run_bass_kernel_spmd

    def chunks(v):
        v = np.asarray(v)
        return np.moveaxis(v.reshape(4, 128, *v.shape[1:]), 0, 1)

    def conv_chunks(v):
        v = np.asarray(v)
        o = np.zeros((128, 6, *v.shape[1:]), v.dtype)
        o[:, 0:4] = chunks(v[0:512])
        o[0:64, 4] = v[512:576]
        o[0:64, 5] = v[576:640]
        return o

    row = lambda v: np.asarray(v).reshape(1, -1)
    keys = np.asarray(L0_ffn_pk_keys).reshape(2, 128, 4, 2, 64).transpose(3, 4, 0, 2, 1).reshape(128, 8, 128)
    arrays = dict(
        x=x, adj=adj, nodemask=np.asarray(nodemask).reshape(_NB, 2, 128).transpose(0, 2, 1),
        tables=np.concatenate([np.asarray(L0_ffn_keys_table), np.asarray(L0_ffn_values_table)], axis=1),
        w0T=np.asarray(L0_gnn_W).T, b0=row(L0_gnn_b), wqpk=L0_ffn_Wq_pk, keysT=keys, wq=L0_ffn_Wq, wo=L0_ffn_Wo,
        w1=np.concatenate([np.asarray(L1_gnn_theta), np.asarray(L1_gnn_W_h), np.asarray(L1_gnn_W_t)], axis=1),
        bt=row(L1_gnn_b_t), wx=L1_ffn_W_x, bx=chunks(L1_ffn_b_x),
        wsliceT=np.tile(np.asarray(L1_ffn_W_slice).T, (2, 1)), bslice=row(L1_ffn_b_slice),
        temp=row(L1_ffn_temperature), wfxT=np.asarray(L1_ffn_W_fx).T, bfx=row(L1_ffn_b_fx),
        inT=np.asarray(L1_ffn_hy_in_w).T, convw=conv_chunks(L1_ffn_hy_conv_w), convb=conv_chunks(L1_ffn_hy_conv_b),
        dtb=row(L1_ffn_hy_dt_bias), alog=row(L1_ffn_hy_A_log),
        drep=chunks(np.repeat(np.asarray(L1_ffn_hy_D), 64)),
        fcdT=np.repeat(np.asarray(L1_ffn_hy_fcD_w), 64, axis=0).T, normw=chunks(L1_ffn_hy_norm_w),
        houtT=np.asarray(L1_ffn_hy_out_w).T, outT=np.asarray(L1_ffn_out_w).T, outb=row(L1_ffn_out_b),
    )
    nc = bacc.Bacc("TRN2", target_bir_lowering=False, num_devices=1)
    ins, args = {}, {}
    for name, a in arrays.items():
        a = np.ascontiguousarray(a)
        ins[f"in_{name}"] = a
        args[name] = nc.dram_tensor(f"in_{name}", a.shape, mybir.dt.from_np(a.dtype), kind="ExternalInput").ap()
    out = nc.dram_tensor("out_x", (_NB, _N, _D), mybir.dt.float32, kind="ExternalOutput").ap()
    build_program(nc, out=out, **args)
    r = run_bass_kernel_spmd(nc, [ins], core_ids=[0])
    return r.results[0]["out_x"]
```
